# Optimizing a Trainium2 kernel written in Bass

```python
import numpy as np
import jax
import jax.numpy as jnp

def _softmax(x, axis=-1):
    return jax.nn.softmax(x, axis=axis)

def _gelu(x):
    return jax.nn.gelu(x, approximate=True)

def _silu(x):
    return jax.nn.silu(x)

def _sigmoid(x):
    return jax.nn.sigmoid(x)

def _layernorm(x, axis=-1, eps=1e-05):
    m = jnp.mean(x, axis=axis, keepdims=True)
    v = jnp.var(x, axis=axis, keepdims=True)
    return (x - m) / jnp.sqrt(v + eps)

def _scatter_add(tgt, idx, src, axis=0):
    return tgt.at[idx].add(src)

def _segment_sum(src, seg, n):
    return jax.ops.segment_sum(src, seg, n)
kernel_name = 'mk_metaformer_d1_conv_nchw128_r2_b13d08'

def setup_inputs(seed: int=0):
    np.random.seed(seed)
    _w = jnp.asarray

    def _rec_inputs():
        import jax
        import jax.numpy as jnp
        _gk = jax.random.key(seed)
        x = -0.000125 + 0.9999 * jax.random.normal(jax.random.fold_in(_gk, 1), (4, 64, 128, 128), jnp.float32)
        return x
    x = _rec_inputs()

    def _L0_conv_setup():
        import jax, jax.numpy as jnp
        import numpy as np
        WS = 8
        HEADS = 4

        def _rel_pos_index(ws):
            coords = np.stack(np.meshgrid(np.arange(ws), np.arange(ws), indexing='ij'))
            flat = coords.reshape(2, -1)
            rel = flat[:, :, None] - flat[:, None, :]
            rel = rel.transpose(1, 2, 0).astype(np.int64)
            rel[:, :, 0] += ws - 1
            rel[:, :, 1] += ws - 1
            rel[:, :, 0] *= 2 * ws - 1
            return rel.sum(-1)
        _REL_IDX = jnp.asarray(_rel_pos_index(WS))
        key = jax.random.key(seed)
        ks = jax.random.split(key, 8)
        dim = 64
        return {'x': jax.random.normal(ks[0], (4, dim, 128, 128), jnp.float32), 'Wq': jax.random.normal(ks[1], (dim, dim), jnp.float32) * 0.02, 'bq': jax.random.normal(ks[2], (dim,), jnp.float32) * 0.02, 'Wkv': jax.random.normal(ks[3], (dim, 2 * dim), jnp.float32) * 0.02, 'bkv': jax.random.normal(ks[4], (2 * dim,), jnp.float32) * 0.02, 'rel_bias': jax.random.normal(ks[5], ((2 * WS - 1) ** 2, HEADS), jnp.float32) * 0.02, 'Wproj': jax.random.normal(ks[6], (dim, dim), jnp.float32) * 0.02, 'bproj': jax.random.normal(ks[7], (dim,), jnp.float32) * 0.02}
    _L0_conv_all = _L0_conv_setup()
    _L0_conv_in = {k: v for k, v in _L0_conv_all.items() if k in ('Wq', 'bq', 'Wkv', 'bkv', 'rel_bias', 'Wproj', 'bproj')}
    del _L0_conv_all

    def _L0_ffn_setup():
        import jax, jax.numpy as jnp
        import numpy as np
        B, N, D, C, E, K = (8, 4096, 64, 64, 8, 2)
        key = jax.random.key(seed)
        k0, k1, k2 = jax.random.split(key, 3)
        x = jax.random.normal(k0, (B, N, D), dtype=jnp.float32)
        router_w = jax.random.normal(k1, (D, E), dtype=jnp.float32) * 0.05
        router_b = jnp.zeros((E,), dtype=jnp.float32)
        expert_w = jax.random.normal(k2, (E, D, C), dtype=jnp.float32) * (1.0 / np.sqrt(D))
        expert_b = jnp.zeros((E, C), dtype=jnp.float32)
        return {'x': x, 'router_w': router_w, 'router_b': router_b, 'expert_w': expert_w, 'expert_b': expert_b}
    _L0_ffn_all = _L0_ffn_setup()
    _L0_ffn_in = {k: v for k, v in _L0_ffn_all.items() if k in ('router_w', 'router_b', 'expert_w', 'expert_b')}
    del _L0_ffn_all
    return {'x': x, 'L0_conv_Wq': _L0_conv_in['Wq'], 'L0_conv_bq': _L0_conv_in['bq'], 'L0_conv_Wkv': _L0_conv_in['Wkv'], 'L0_conv_bkv': _L0_conv_in['bkv'], 'L0_conv_rel_bias': _L0_conv_in['rel_bias'], 'L0_conv_Wproj': _L0_conv_in['Wproj'], 'L0_conv_bproj': _L0_conv_in['bproj'], 'L0_ffn_router_w': _L0_ffn_in['router_w'], 'L0_ffn_router_b': _L0_ffn_in['router_b'], 'L0_ffn_expert_w': _L0_ffn_in['expert_w'], 'L0_ffn_expert_b': _L0_ffn_in['expert_b']}

def reference(x, L0_conv_Wq, L0_conv_bq, L0_conv_Wkv, L0_conv_bkv, L0_conv_rel_bias, L0_conv_Wproj, L0_conv_bproj, L0_ffn_router_w, L0_ffn_router_b, L0_ffn_expert_w, L0_ffn_expert_b):
    import jax
    import jax.numpy as jnp

    def _L0_conv_ref(x, Wq, bq, Wkv, bkv, rel_bias, Wproj, bproj):
        import jax, jax.numpy as jnp
        import numpy as np
        WS = 8
        HEADS = 4

        def _rel_pos_index(ws):
            coords = np.stack(np.meshgrid(np.arange(ws), np.arange(ws), indexing='ij'))
            flat = coords.reshape(2, -1)
            rel = flat[:, :, None] - flat[:, None, :]
            rel = rel.transpose(1, 2, 0).astype(np.int64)
            rel[:, :, 0] += ws - 1
            rel[:, :, 1] += ws - 1
            rel[:, :, 0] *= 2 * ws - 1
            return rel.sum(-1)
        _REL_IDX = jnp.asarray(_rel_pos_index(WS))
        B, C, H, W = x.shape
        ws, nh = (WS, HEADS)
        N = ws * ws
        dh = C // nh
        xw = x.reshape(B, H // ws, ws, W // ws, ws, C)
        xw = xw.transpose(0, 1, 3, 2, 4, 5).reshape(-1, N, C)
        B_ = xw.shape[0]
        q = (xw @ Wq + bq).reshape(B_, N, nh, dh).transpose(0, 2, 1, 3)
        kv = (xw @ Wkv + bkv).reshape(B_, N, 2, nh, dh).transpose(2, 0, 3, 1, 4)
        k, v = (kv[0], kv[1])
        scale = dh ** (-0.5)
        attn = jnp.einsum('bhnd,bhmd->bhnm', q * scale, k)
        bias = rel_bias[_REL_IDX.reshape(-1)].reshape(N, N, nh).transpose(2, 0, 1)
        attn = jax.nn.softmax(attn + bias[None], axis=-1)
        out = jnp.einsum('bhnm,bhmd->bhnd', attn, v)
        out = out.transpose(0, 2, 1, 3).reshape(B_, N, C)
        out = out @ Wproj + bproj
        out = out.reshape(B, H // ws, W // ws, ws, ws, C)
        out = out.transpose(0, 1, 3, 2, 4, 5).reshape(B, H, W, C)
        return out.transpose(0, 3, 1, 2)

    def _L0_ffn_ref(x, router_w, router_b, expert_w, expert_b):
        import jax, jax.numpy as jnp
        import numpy as np
        B, N, D, C, E, K = (8, 4096, 64, 64, 8, 2)
        router_probs = jax.nn.softmax(x @ router_w + router_b, axis=-1)
        top_p, top_i = jax.lax.top_k(router_probs, K)
        top_p = top_p / jnp.sum(top_p, axis=-1, keepdims=True)
        expert_out = jnp.einsum('bnd,edc->bnec', x, expert_w) + expert_b
        gathered = jnp.take_along_axis(expert_out, top_i[..., None], axis=2)
        return jnp.einsum('bnk,bnkc->bnc', top_p, gathered)

    def _gn(v, G=32, eps=1e-05):
        B_, C_, H_, W_ = v.shape
        g = v.reshape(B_, G, C_ // G, H_, W_)
        m = jnp.mean(g, axis=(2, 3, 4), keepdims=True)
        s = jnp.var(g, axis=(2, 3, 4), keepdims=True)
        return ((g - m) / jnp.sqrt(s + eps)).reshape(v.shape)

    def _ln_c(v, eps=1e-06):
        m = jnp.mean(v, axis=1, keepdims=True)
        s = jnp.var(v, axis=1, keepdims=True)
        return (v - m) / jnp.sqrt(s + eps)

    def _ln_t(v, eps=1e-05):
        m = jnp.mean(v, axis=-1, keepdims=True)
        s = jnp.var(v, axis=-1, keepdims=True)
        return (v - m) / jnp.sqrt(s + eps)

    def _to_tokens(v):
        B_, C_, H_, W_ = v.shape
        return v.reshape(B_, C_, H_ * W_).transpose(0, 2, 1)

    def _from_tokens(t, like):
        B_, C_, H_, W_ = like.shape
        return t.transpose(0, 2, 1).reshape(B_, C_, H_, W_)
    x = x + _L0_conv_ref(_ln_c(x), L0_conv_Wq, L0_conv_bq, L0_conv_Wkv, L0_conv_bkv, L0_conv_rel_bias, L0_conv_Wproj, L0_conv_bproj)
    t = _to_tokens(x)
    t = t + _L0_ffn_ref(_ln_t(t), L0_ffn_router_w, L0_ffn_router_b, L0_ffn_expert_w, L0_ffn_expert_b)
    x = _from_tokens(t, x)
    return x

_drawn_inputs = setup_inputs


def setup_inputs(seed=0):
    import zlib

    import numpy as np

    out = dict(_drawn_inputs(seed))
    spreads = {'L0_ffn_router_b': (0.0, 0.1), 'L0_ffn_expert_b': (0.0, 0.1)}
    factors = {'L0_conv_Wq': 31.734, 'L0_conv_bq': 197.63, 'L0_conv_rel_bias': 46.251}
    for name, (base, spread) in spreads.items():
        noise = np.random.default_rng([zlib.crc32(name.encode()), seed]).standard_normal(out[name].shape)
        drawn = base * np.exp(spread * noise) if base else spread * noise
        out[name] = jnp.asarray(drawn.astype(out[name].dtype))
    for name, factor in factors.items():
        out[name] = (out[name] * factor).astype(out[name].dtype)
    return out
```

```python
from contextlib import ExitStack

import numpy as np

import concourse.bass as bass
from concourse import mybir

F32 = mybir.dt.float32
BF16 = mybir.dt.bfloat16
ALU = mybir.AluOpType
ACT = mybir.ActivationFunctionType
AX = mybir.AxisListType

BATCH, C, H, W = 4, 64, 128, 128
P = 128
HEADS, DH = 4, 16
WS = 8
NTOK = WS * WS
STRIPS = C // 4
PAIRS = 8
UNITS = PAIRS // 2
BANK = 512
EXPERTS = 8
ROWS = 8
GROUPS = C // 4
RING = 4
PVW = 96
PARTS = 3
GROWS = PARTS * 2 * EXPERTS
LN_C_EPS, LN_T_EPS = 1e-6, 1e-5


class Sem:

    def __init__(self, sem, per=1, primed=0):
        self.sem, self.per, self.primed = sem, per, primed

    def at(self, n, k=0):
        return n * self.per + (k + self.primed)


def build(nc, x, wqkv, qkvb, kmask, kbias, wproj, wrout, brout, wexp, bexp, relb, ident, sel, rank, out):
    ctx = ExitStack()
    with ctx:
        def sb(name, shape, dt=F32):
            return ctx.enter_context(nc.sbuf_tensor(name, shape, dt))

        def sem(name, per=1, primed=0):
            s = Sem(ctx.enter_context(nc.semaphore(name)), per, primed)
            primed_sems.extend([s] * primed)
            return s

        primed_sems = []

        w_qkv = sb("w_qkv", [P, 2, 3, C])
        b_qkv = sb("b_qkv", [P, 3])
        q_bias = sb("q_bias", [P, 1])
        k_mask = sb("k_mask", [P, HEADS])
        k_bias = sb("k_bias", [P, HEADS])
        w_proj = sb("w_proj", [C + 1, C])
        w_rout = sb("w_rout", [P, 2 * EXPERTS])
        b_rout = sb("b_rout", [P, ROWS, EXPERTS])
        w_exp = sb("w_exp", [P, EXPERTS, P])
        b_exp = sb("b_exp", [GROWS, P])
        b_exp_part = sb("b_exp_part", [GROWS, PARTS, P], BF16)
        rel = sb("rel", [P, HEADS * NTOK])
        idn = sb("idn", [P, P])
        idn16 = sb("idn16", [P, P], BF16)
        gate_sel = sb("gate_sel", [GROWS, EXPERTS, P])
        gate_sel16 = sb("gate_sel16", [GROWS, EXPERTS, P], BF16)
        e_rank = sb("e_rank", [P, ROWS, EXPERTS])
        mhalf = sb("mhalf", [P, H])

        x_in = sb("x_in", [P, RING, 4, W])
        xt = sb("xt", [P, C, H])
        x_sq = sb("x_sq", [P, 2, 4, H])
        sums = sb("sums", [P, H, GROUPS])
        sums2 = sb("sums2", [P, H, GROUPS])
        st = sb("st", [P, 6, H])

        xn = sb("xn", [P, 4, H])
        q_bd = sb("q_bd", [P, PAIRS, 2 * NTOK])
        k_m = sb("k_m", [P, PAIRS, HEADS, NTOK])
        v_t = sb("v_t", [P, PAIRS + 1, NTOK])
        v_bd = sb("v_bd", [P, PAIRS, 2, PVW])
        prob = sb("prob", [P, UNITS, 2, HEADS, NTOK])
        mx = sb("mx", [P, UNITS, 2 * HEADS])
        prob_t = sb("prob_t", [P, 2, 2, 2, P])
        r_sum = sb("r_sum", [P, UNITS, 4, 2])
        o_n = sb("o_n", [P, PAIRS, C])
        o_t = sb("o_t", [C + 1, ROWS, W])
        x2 = sb("x2", [P, ROWS, C])

        ln = sb("ln", [P, 4, ROWS])
        xc = sb("xc", [P, ROWS, C])
        xc2 = sb("xc2", [P, ROWS, C])
        t_n = sb("t_n", [P, ROWS, C])
        t_t = sb("t_t", [P, 4, P])
        rt = sb("rt", [P, 8, ROWS, EXPERTS])
        rs = sb("rs", [P, 8, ROWS])
        g3 = sb("g3", [P, 4, PARTS, 2 * EXPERTS], BF16)
        g_t = sb("g_t", [GROWS, BANK], BF16)
        t_g = sb("t_g", [P, 2, BANK])
        y_out = sb("y_out", [P, 4, W])

        bank = [ctx.enter_context(nc.psum_tensor(f"bank{i}", [P, BANK], F32)) for i in range(8)]
        B_S = bank[0:2]
        B_T = bank[2:4]
        B_M = bank[4]
        B_G = bank[5:7]
        B_Y = bank[7]

        loads = ctx.enter_context(nc.semaphore("weights_loaded"))
        x_loaded = [Sem(ctx.enter_context(nc.semaphore(f"x_loaded{r}"))) for r in range(RING)]
        passed = ctx.enter_context(nc.semaphore("passed"))
        stored = ctx.enter_context(nc.semaphore("stored"))
        set_pool = sem("set_pool")
        set_dve = sem("set_dve")
        set_act = sem("set_act")
        x_turned = sem("x_turned")
        xt_ready = sem("xt_ready", primed=1)
        sq_ready = sem("sq_ready")
        part_sums = sem("part_sums", 2, primed=1)
        stat = sem("stat", 6)
        rstd_ready = sem("rstd_ready")
        mr_ready = sem("mr_ready")

        xn_ready = sem("xn_ready", 2)
        qkv_done = sem("qkv_done", 3, primed=1)
        q_ready = sem("q_ready", 4)
        k_ready = sem("k_ready", 4)
        v_ready = sem("v_ready", 2)
        vrow_done = sem("vrow_done", 2)
        vbd_ready = sem("vbd_ready", 10)
        s_done = sem("s_done", UNITS)
        s_biased = sem("s_biased", UNITS, primed=1)
        mx_ready = sem("mx_ready", UNITS)
        s_shifted = sem("s_shifted", UNITS)
        p_ready = sem("p_ready", UNITS)
        pt_done = sem("pt_done", UNITS)
        pt_ready = sem("pt_ready", UNITS)
        pv_done = sem("pv_done", UNITS, primed=1)
        rsum_ready = sem("rsum_ready", UNITS)
        on_ready = sem("on_ready", 2 * UNITS)
        ot_done = sem("ot_done", 2)
        ot_ready = sem("ot_ready", 4, primed=1)
        proj_done = sem("proj_done")
        x2_ready = sem("x2_ready", primed=1)

        lsum = sem("lsum", 2)
        xc_ready = sem("xc_ready")
        xc2_ready = sem("xc2_ready")
        lvar = sem("lvar", 2)
        lrstd = sem("lrstd")
        t_ready = sem("t_ready")
        tt_done = sem("tt_done")
        tt_ready = sem("tt_ready")
        logits_done = sem("logits_done")
        route = sem("route", 23)
        e_ready = sem("e_ready")
        gt_done = sem("gt_done")
        gt_ready = sem("gt_ready")
        gate_done = sem("gate_done", EXPERTS)
        tg_ready = sem("tg_ready", EXPERTS, primed=1)
        y_done = sem("y_done", EXPERTS, primed=1)
        y_ready = sem("y_ready", primed=1)

        consts = [(w_qkv, wqkv), (b_qkv, qkvb), (k_mask, kmask), (k_bias, kbias), (w_proj, wproj), (w_rout, wrout),
                  (b_rout, brout), (w_exp, wexp), (b_exp, bexp), (rel, relb), (idn, ident),
                  (gate_sel, sel), (e_rank, rank)]
        ALL_LOADED = 16 * len(consts)

        block = ctx.enter_context(nc.Block())

        def turned(ap):
            return ap.rearrange("p (a v l) -> p v a l", v=PAIRS, l=4)

        def slots(eng, slot, phase_a):
            with eng.Fori(0, BATCH) as b:
                phase_a(b)
                slot((b * STRIPS, 0), None)
                with eng.Fori(1, STRIPS) as s:
                    slot((b * STRIPS + s, s), (b * STRIPS + s - 1, b, s - 1))
                slot(None, (b * STRIPS + STRIPS - 1, b, STRIPS - 1))

        @block.sync
        def _(sp):
            for s in primed_sems:
                sp.sem_inc(s.sem, 1)
            sp.sem_inc(stored, 1)
            for dst, src in consts:
                sp.dma_start(dst[tuple(slice(None) for _ in dst.shape)], src).then_inc(loads, 16)
            xg = x.rearrange("b (q c) h w -> (b q) h c w", c=4)
            for r in range(RING):
                sp.dma_start(x_in[:, r], xg[r]).then_inc(x_loaded[r].sem, 16)
            with sp.Fori(0, BATCH * GROUPS // RING - 1) as t:
                for r in range(RING):
                    sp.wait_ge(x_turned.sem, x_turned.at(t * RING, r + 1))
                    sp.dma_start(x_in[:, r], xg[bass.ds(t * RING + RING + r, 1)].rearrange("o h c w -> h (o c) w")
                                 ).then_inc(x_loaded[r].sem, 16)

        @block.tensor
        def _(pe):
            mm, tr = nc.tensor.matmul, nc.tensor.transpose
            pe.wait_ge(loads, ALL_LOADED)
            pe.wait_ge(set_dve.sem, set_dve.at(0, SET_DVE))
            pe.wait_ge(set_pool.sem, set_pool.at(0, SET_POOL))

            def phase_a(b):
                with pe.Fori(0, GROUPS // RING) as t:
                    for r in range(RING):
                        pe.wait_ge(x_loaded[r].sem, (b * (GROUPS // RING) + t + 1) * 16)
                        if r == 0:
                            pe.wait_ge(s_biased.sem, s_biased.at(b * STRIPS))
                        pe.wait_ge(xt_ready.sem, xt_ready.at(b * GROUPS + t * RING, max(r - 1, 0)))
                        for c in range(4):
                            last = tr(B_S[r % 2][:, c * H:(c + 1) * H], x_in[:, r, c, :], idn[:, :])
                        last.then_inc(x_turned.sem, 1)

            def project(g, i, dst):
                for half in range(2):
                    for ab in range(2):
                        src = xn[:, :, :].rearrange("p c (hh ab l) -> p (c hh) ab l", ab=2, l=32)[:, :, ab, :]
                        last = mm(dst[C * ab:C * ab + C, 256 * half:256 * half + 256], w_qkv[:, half, i, :], src,
                                  start=True, stop=True, skip_group_check=True)
                last.then_inc(qkv_done.sem, 1)

            def turn_values(g, u, dst):
                for n in range(4):
                    v = 4 * u + n
                    last = tr(dst[:, n * P:(n + 1) * P], v_t[:, v:v + 2, :].rearrange("p v t -> p (v t)"), idn[:, :])
                last.then_inc(vrow_done.sem, 1)

            def scores(g, i):
                pe.wait_ge(s_biased.sem, s_biased.at(g, max(i - 1, 0)))
                for n in range(2):
                    v = 2 * i + n
                    last = mm(B_S[i % 2][:, n * 256:(n + 1) * 256], q_bd[:, v, :],
                              k_m[:, v, :, :].rearrange("p h k -> p (h k)"), start=True, stop=True,
                              skip_group_check=True)
                last.then_inc(s_done.sem, 1)

            def turn_probs(g, i):
                pe.wait_ge(p_ready.sem, p_ready.at(g, i + 1))
                if i == 0:
                    pe.wait_ge(vbd_ready.sem, vbd_ready.at(g, 10))
                elif i >= 2:
                    pe.wait_ge(pt_ready.sem, pt_ready.at(g, i - 1))
                for n in range(2):
                    for hp in range(2):
                        at = (2 * n + hp) * P
                        last = tr(B_T[i % 2][:, at:at + P],
                                  prob[:, i, n, 2 * hp:2 * hp + 2, :].rearrange("p h k -> p (h k)"), idn[:, :])
                last.then_inc(pt_done.sem, 1)

            def values(g, i):
                pe.wait_ge(pt_ready.sem, pt_ready.at(g, i + 1))
                if i:
                    pe.wait_ge(on_ready.sem, on_ready.at(g, 2 * i))
                for n in range(2):
                    for hp in range(2):
                        at = (2 * n + hp) * PVW
                        last = mm(B_M[:, at:at + PVW], prob_t[:, i % 2, n, hp, :], v_bd[:, 2 * i + n, hp, :],
                                  start=True, stop=True, skip_group_check=True)
                last.then_inc(pv_done.sem, 1)

            def turn_outputs(g, u):
                pe.wait_ge(on_ready.sem, on_ready.at(g, 4 * u + 4))
                pe.wait_ge(pt_ready.sem, pt_ready.at(g, 3 + u))
                pe.sem_inc(passed, 1)
                for n in range(4):
                    last = tr(B_T[u][0:C, n * P:(n + 1) * P], o_n[:, 4 * u + n, :], idn[:, :])
                last.then_inc(ot_done.sem, 1)

            def project_out(g):
                pe.wait_ge(ot_ready.sem, ot_ready.at(g, 4))
                for r in range(ROWS):
                    at = (r % 4 * 2 + r // 4) * C
                    last = mm(B_M[:, at:at + C], o_t[:, r, :], w_proj[:, :], start=True, stop=True,
                              skip_group_check=True)
                last.then_inc(proj_done.sem, 1)

            def turn_tokens(g):
                pe.wait_ge(t_ready.sem, t_ready.at(g, 1))
                pe.wait_ge(tg_ready.sem, tg_ready.at(g))
                for k in range(4):
                    src = t_n[:, 2 * k:2 * k + 2, :].rearrange("p a c -> p (a c)")
                    last = tr(B_G[0][:, k * P:(k + 1) * P], src, idn[:, :])
                last.then_inc(tt_done.sem, 1)

            def logits(g):
                pe.wait_ge(tt_ready.sem, tt_ready.at(g, 1))
                for k in range(4):
                    last = mm(B_G[1][:, k * 16:(k + 1) * 16], t_t[:, k, :], w_rout[:, :], start=True, stop=True,
                              skip_group_check=True)
                last.then_inc(logits_done.sem, 1)

            def residual(g):
                pe.wait_ge(y_ready.sem, y_ready.at(g))
                for k in range(4):
                    src = x2[:, 2 * k:2 * k + 2, :].rearrange("p a c -> p (a c)")
                    mm(B_Y[:, k * P:(k + 1) * P], src, idn[:, :], start=(k == 0), stop=False, skip_group_check=True)

            def turn_gates(g):
                pe.wait_ge(route.sem, route.at(g, route.per))
                pe.sem_inc(passed, 1)
                gt16 = B_G[0][:, :].bitcast(BF16)
                for k in range(4):
                    last = tr(gt16[0:GROWS, k * P:(k + 1) * P], g3[:, k].rearrange("p a e -> p (a e)"), idn16[:, :])
                last.then_inc(gt_done.sem, 1)

            def expert_bias(g):
                pe.wait_ge(gt_ready.sem, gt_ready.at(g, 1))
                for part in range(PARTS):
                    mm(B_Y[:, :], b_exp_part[:, part, :], g_t[:, :], start=False, stop=False, skip_group_check=True)

            def gates(g, e):
                if e >= 2:
                    pe.wait_ge(tg_ready.sem, tg_ready.at(g, e - 1))
                mm(B_G[e % 2][:, :], gate_sel16[:, e, :], g_t[:, :], start=True, stop=True).then_inc(gate_done.sem, 1)

            def expert(g, e):
                pe.wait_ge(tg_ready.sem, tg_ready.at(g, e + 1))
                mm(B_Y[:, :], w_exp[:, e, :], t_g[:, e % 2, :], start=False, stop=(e == EXPERTS - 1),
                             skip_group_check=True).then_inc(y_done.sem, 1)

            def slot(front, back):
                def f(step, *args):
                    if front:
                        step(front[0], *args)

                def k(step, *args):
                    if back:
                        step(back[0], *args)

                if front:
                    g = front[0]
                    pe.wait_ge(xn_ready.sem, xn_ready.at(g, 2))
                    pe.wait_ge(x2_ready.sem, x2_ready.at(g))
                    project(g, 0, B_M)
                    pe.wait_ge(ot_ready.sem, ot_ready.at(g))
                    project(g, 1, B_T[0])
                    project(g, 2, B_T[1])
                    pe.wait_ge(v_ready.sem, v_ready.at(g, 2))
                    pe.wait_ge(q_ready.sem, q_ready.at(g, 4))
                    turn_values(g, 0, B_M)
                    pe.wait_ge(k_ready.sem, k_ready.at(g, 4))
                    turn_values(g, 1, B_T[0])
                f(scores, 0)
                f(scores, 1)
                k(turn_tokens)
                f(scores, 2)
                k(logits)
                f(scores, 3)
                f(turn_probs, 0)
                k(residual)
                f(turn_probs, 1)
                f(values, 0)
                f(turn_probs, 2)
                k(turn_gates)
                k(expert_bias)
                k(gates, 0)
                k(gates, 1)
                k(expert, 0)
                f(values, 1)
                f(turn_probs, 3)
                k(gates, 2)
                k(expert, 1)
                f(values, 2)
                k(gates, 3)
                k(expert, 2)
                f(values, 3)
                k(gates, 4)
                k(expert, 3)
                f(turn_outputs, 0)
                f(turn_outputs, 1)
                k(gates, 5)
                k(expert, 4)
                k(gates, 6)
                k(expert, 5)
                f(project_out)
                k(gates, 7)
                k(expert, 6)
                k(expert, 7)

            slots(pe, slot, phase_a)

        @block.scalar
        def _(act):
            A = nc.scalar.activation
            act.wait_ge(loads, ALL_LOADED)
            A(q_bias[:, :], b_qkv[:, 0:1], ACT.Copy, scale=float(DH) ** -0.5).then_inc(set_act.sem, 1)
            act.wait_ge(set_act.sem, set_act.at(0, 1))
            act.wait_ge(set_pool.sem, set_pool.at(0, SET_POOL))

            def phase_a(b):
                act.wait_ge(x2_ready.sem, x2_ready.at(b * STRIPS))
                with act.Fori(0, GROUPS // 2) as t:
                    for r in range(2):
                        n = b * GROUPS + t * 2
                        dst = xt[:, bass.ds(t * 8 + 4 * r, 4), :]
                        act.wait_ge(x_turned.sem, x_turned.at(n, r + 1))
                        act.sem_inc(passed, 1)
                        A(dst, B_S[r][:, :].rearrange("p (c h) -> p c h", c=4), ACT.Copy).then_inc(xt_ready.sem, 1)
                        act.wait_ge(xt_ready.sem, xt_ready.at(n, r + 1))
                        act.wait_ge(part_sums.sem, part_sums.at(n, 0))
                        act.sem_inc(passed, 1)
                        A(x_sq[:, r], dst, ACT.Square).then_inc(sq_ready.sem, 1)

            def copy_qkv(g):
                act.wait_ge(qkv_done.sem, qkv_done.at(g, 1))
                for ab in range(2):
                    rows = slice(C * ab, C * ab + C)
                    for half in range(2):
                        A(
                            q_bd[rows, :, ab * NTOK:(ab + 1) * NTOK].rearrange("p v (r l a) -> p v r l a", a=2, l=4)[
                                :, :, :, :, half],
                            turned(B_M[rows, 256 * half:256 * half + 256]), ACT.Identity, bias=q_bias[rows, :],
                            scale=float(DH) ** -0.5).then_inc(q_ready.sem, 1)
                act.wait_ge(qkv_done.sem, qkv_done.at(g, 2))
                for h in range(HEADS):
                    A(k_m[:, :, h, :].rearrange("p v (a l) -> p v a l", l=4), turned(B_T[0][:, :]),
                                 ACT.Identity, bias=k_bias[:, h:h + 1], scale=k_mask[:, h:h + 1]).then_inc(k_ready.sem, 1)
                act.wait_ge(qkv_done.sem, qkv_done.at(g, 3))
                A(v_t[:, 0:PAIRS, :].rearrange("p v (a l) -> p v a l", l=4), turned(B_T[1][:, :]),
                             ACT.Identity, bias=b_qkv[:, 2:3]).then_inc(v_ready.sem, 1)
                A(v_t[:, PAIRS, :].rearrange("p (a l) -> p a l", l=4), turned(B_T[1][:, :])[:, 0],
                             ACT.Identity, bias=b_qkv[:, 2:3]).then_inc(v_ready.sem, 1)

            def exps(g, i):
                act.wait_ge(s_shifted.sem, s_shifted.at(g, i + 1))
                A(prob[:, i], prob[:, i], ACT.Exp).then_inc(p_ready.sem, 1)

            def copy_probs(g, i):
                act.wait_ge(pt_done.sem, pt_done.at(g, i + 1))
                act.wait_ge(pv_done.sem, pv_done.at(g, max(i - 1, 0)))
                A(prob_t[:, i % 2].rearrange("p n h q -> p (n h q)"), B_T[i % 2][:, :], ACT.Copy).then_inc(pt_ready.sem, 1)

            def copy_outputs(g, u):
                act.wait_ge(ot_done.sem, ot_done.at(g, u + 1))
                for ab in range(2):
                    at = (PAIRS * ab + 4 * u) * WS
                    A(
                        o_t[0:C, :, at:at + 4 * WS].rearrange("c r (v s) -> c v r s", s=WS),
                        B_T[u][0:C, :].rearrange("c (v ab r s) -> c ab v r s", v=4, ab=2, s=WS)[:, ab], ACT.Copy).then_inc(ot_ready.sem, 1)

            def square(g):
                act.wait_ge(xc_ready.sem, xc_ready.at(g, 1))
                A(xc2[:, :, :], xc[:, :, :], ACT.Square).then_inc(xc2_ready.sem, 1)

            def copy_tokens(g):
                act.wait_ge(tt_done.sem, tt_done.at(g, 1))
                A(t_t[:, :, :].rearrange("p k w -> p (k w)"), B_G[0][:, :], ACT.Copy).then_inc(tt_ready.sem, 1)

            def gate_exp(g):
                act.wait_ge(route.sem, route.at(g, ROUTE_GAP))
                A(rs[:, 4, :], rs[:, 3, :], ACT.Exp).then_inc(e_ready.sem, 1)

            def copy_gates(g):
                act.wait_ge(gt_done.sem, gt_done.at(g, 1))
                A(g_t[:, :], B_G[0][:, :].bitcast(BF16)[0:GROWS, 0:BANK], ACT.Copy).then_inc(gt_ready.sem, 1)

            def store(g, b, s):
                act.wait_ge(y_done.sem, y_done.at(g, EXPERTS))
                act.wait_ge(stored, g * 32 + 1)
                A(y_out[:, :, :].rearrange("p k w -> p (k w)"), B_Y[:, :], ACT.Copy).then_inc(y_ready.sem, 1)
                act.wait_ge(y_ready.sem, y_ready.at(g, 1))
                for a in range(2):
                    dst = out[bass.ds(b, 1), :, bass.ds(s * ROWS + 4 * a, 4), :].rearrange("o c k w -> (o c) k w")
                    act.dma_start(dst, y_out[C * a:C * a + C]).then_inc(stored, 16)

            def slot(front, back):
                def f(step, *args):
                    if front:
                        step(front[0], *args)

                def k(step, *args):
                    if back:
                        step(back[0], *args)

                k(square)
                f(copy_qkv)
                f(exps, 0)
                k(copy_tokens)
                f(exps, 1)
                f(exps, 2)
                f(exps, 3)
                f(copy_probs, 0)
                f(copy_probs, 1)
                k(gate_exp)
                f(copy_probs, 2)
                k(copy_gates)
                f(copy_probs, 3)
                f(copy_outputs, 0)
                f(copy_outputs, 1)
                k(store, *(back or (0, 0, 0))[1:])

            slots(act, slot, phase_a)
            act.wait_ge(stored, BATCH * STRIPS * 32 + 1)

        @block.vector
        def _(dve):
            V = nc.vector
            dve.wait_ge(loads, ALL_LOADED)
            V.memset(v_bd[:, :, :, :], 0.0).then_inc(set_dve.sem, 1)
            dve.wait_ge(set_dve.sem, 1)
            for j in range(2):
                V.memset(v_bd[C * j:C * j + C, :, :, 64 + j:65 + j], 1.0).then_inc(set_dve.sem, 1)
            V.tensor_copy(idn16[:, :], idn[:, :]).then_inc(set_dve.sem, 1)
            V.tensor_copy(gate_sel16[:, :, :], gate_sel[:, :, :]).then_inc(set_dve.sem, 1)
            V.tensor_copy(b_exp_part[:, 0, :], b_exp[:, :]).then_inc(set_dve.sem, 1)
            for part in range(1, PARTS):
                dve.wait_ge(set_dve.sem, 4 + 2 * part)
                V.tensor_tensor(b_exp[:, :], b_exp[:, :], b_exp_part[:, part - 1, :], ALU.subtract).then_inc(set_dve.sem, 1)
                dve.wait_ge(set_dve.sem, 5 + 2 * part)
                V.tensor_copy(b_exp_part[:, part, :], b_exp[:, :]).then_inc(set_dve.sem, 1)

            def phase_a(b):
                with dve.Fori(0, GROUPS // 2) as t:
                    for r in range(2):
                        n = b * GROUPS + t * 2
                        dve.wait_ge(xt_ready.sem, xt_ready.at(n, r + 1))
                        dst = sums[:, :, bass.ds(t * 2 + r, 1)].rearrange("p h o -> p (h o)")
                        V.tensor_reduce(
                            dst, xt[:, bass.ds(t * 8 + 4 * r, 4), :].rearrange("p c h -> p h c"), AX.X, ALU.add).then_inc(part_sums.sem, 1)
                        dve.wait_ge(sq_ready.sem, sq_ready.at(n, r + 1))
                        dst = sums2[:, :, bass.ds(t * 2 + r, 1)].rearrange("p h o -> p (h o)")
                        V.tensor_reduce(dst, x_sq[:, r].rearrange("p c h -> p h c"), AX.X, ALU.add).then_inc(part_sums.sem, 1)
                dve.wait_ge(part_sums.sem, part_sums.at(b * GROUPS + GROUPS))
                V.tensor_reduce(st[:, 0, :], sums[:, :, :], AX.X, ALU.add).then_inc(stat.sem, 1)
                V.tensor_reduce(st[:, 1, :], sums2[:, :, :], AX.X, ALU.add).then_inc(stat.sem, 1)
                dve.wait_ge(stat.sem, stat.at(b, 2))
                V.tensor_scalar(st[:, 2, :], st[:, 0, :], 1.0 / C, None, ALU.mult).then_inc(stat.sem, 1)
                dve.wait_ge(stat.sem, stat.at(b, 3))
                V.tensor_tensor(st[:, 3, :], st[:, 2, :], st[:, 2, :], ALU.mult).then_inc(stat.sem, 1)
                dve.wait_ge(stat.sem, stat.at(b, 4))
                V.scalar_tensor_tensor(out=st[:, 4, :], in0=st[:, 1, :], scalar=1.0 / C, in1=st[:, 3, :],
                                               op0=ALU.mult, op1=ALU.subtract).then_inc(stat.sem, 1)
                dve.wait_ge(stat.sem, stat.at(b, 5))
                V.tensor_scalar(st[:, 4, :], st[:, 4, :], 0.0, LN_C_EPS, ALU.max, ALU.add).then_inc(stat.sem, 1)
                dve.wait_ge(rstd_ready.sem, rstd_ready.at(b, 1))
                V.tensor_tensor(st[:, 0, :], st[:, 2, :], st[:, 5, :], ALU.mult).then_inc(mr_ready.sem, 1)

            def spread_values(g, u):
                dve.wait_ge(vrow_done.sem, vrow_done.at(g, u + 1))
                src = (B_M, B_T[0])[u]
                runs = [(0, 0, 4, 4 * u), (1, 0, 4, 1)] if u == 0 else [(0, 0, 4, 4), (1, 0, 3, 5), (1, 3, 1, 0)]
                for j, n0, count, v0 in runs:
                    rows = slice(C * j, C * j + C)
                    for hp in range(2):
                        at = (2 * hp + j) * DH
                        V.tensor_copy(
                            v_bd[rows, v0:v0 + count, hp, 0:64].rearrange("p v (ab c) -> p v ab c", ab=2)[
                                :, :, :, j * DH:(j + 1) * DH],
                            src[rows, :].rearrange("p (v ab c) -> p v ab c", v=4, ab=2)[
                                :, n0:n0 + count, :, at:at + DH]).then_inc(vbd_ready.sem, 1)

            def bias_and_max(g, i):
                dve.wait_ge(s_done.sem, s_done.at(g, i + 1))
                V.tensor_tensor(
                    prob[:, i].rearrange("p n h k -> p n (h k)"), B_S[i % 2][:, :].rearrange("p (n c) -> p n c", n=2),
                    rel[:, :].unsqueeze(1).broadcast_to([P, 2, HEADS * NTOK]), ALU.add).then_inc(s_biased.sem, 1)
                dve.wait_ge(s_biased.sem, s_biased.at(g, i + 1))
                V.tensor_reduce(mx[:, i, :], prob[:, i].rearrange("p n h k -> p (n h) k"), AX.X, ALU.max).then_inc(mx_ready.sem, 1)

            def normalise(g, i):
                dve.wait_ge(pv_done.sem, pv_done.at(g, i + 1))
                ps = B_M[:, 0:4 * PVW].rearrange("p (m c) -> p m c", c=PVW)
                V.reciprocal(r_sum[:, i], ps[:, :, 64:66]).then_inc(rsum_ready.sem, 1)
                dve.wait_ge(rsum_ready.sem, rsum_ready.at(g, i + 1))
                for ab in range(2):
                    rows = slice(C * ab, C * ab + C)
                    V.tensor_tensor(
                        o_n[rows, 2 * i:2 * i + 2, :].rearrange("p n (h j d) -> p (n h) j d", h=2, j=2),
                        ps[rows, :, 32 * ab:32 * ab + 32].rearrange("p m (j d) -> p m j d", j=2),
                        r_sum[rows, i].unsqueeze(3).broadcast_to([C, 4, 2, DH]), ALU.mult).then_inc(on_ready.sem, 1)

            def add_input(g, s):
                dve.wait_ge(proj_done.sem, proj_done.at(g, 1))
                V.tensor_tensor(
                    x2[:, :, :].rearrange("p (k a) c -> p k a c", a=2),
                    B_M[:, :].rearrange("p (k a c) -> p k a c", a=2, c=C),
                    xt[:, :, bass.ds(s * ROWS, ROWS)].rearrange("p c (a k) -> p k a c", a=2), ALU.add).then_inc(x2_ready.sem, 1)

            def token_mean(g):
                dve.wait_ge(x2_ready.sem, x2_ready.at(g, 1))
                V.tensor_reduce(ln[:, 0, :], x2[:, :, :], AX.X, ALU.add).then_inc(lsum.sem, 1)
                dve.wait_ge(lsum.sem, lsum.at(g, 1))
                V.tensor_scalar(ln[:, 1, :], ln[:, 0, :], 1.0 / C, None, ALU.mult).then_inc(lsum.sem, 1)

            def token_variance(g):
                dve.wait_ge(xc2_ready.sem, xc2_ready.at(g, 1))
                V.tensor_reduce(ln[:, 2, :], xc2[:, :, :], AX.X, ALU.add).then_inc(lvar.sem, 1)
                dve.wait_ge(lvar.sem, lvar.at(g, 1))
                V.tensor_scalar(ln[:, 2, :], ln[:, 2, :], 1.0 / C, LN_T_EPS, ALU.mult, ALU.add).then_inc(lvar.sem, 1)

            def routing(g):
                dve.wait_ge(logits_done.sem, logits_done.at(g, 1))
                def each(v):
                    return v.unsqueeze(2).broadcast_to([P, ROWS, EXPERTS])

                lg, hot, first, rest, second = (rt[:, n] for n in range(5))
                V.tensor_tensor(lg, B_G[1][:, 0:64].rearrange("p (r e) -> p r e", e=EXPERTS), b_rout[:, :, :], ALU.add).then_inc(route.sem, 1)
                dve.wait_ge(route.sem, route.at(g, 1))

                V.tensor_reduce(rs[:, 0, :], lg, AX.X, ALU.max).then_inc(route.sem, 1)
                dve.wait_ge(route.sem, route.at(g, 2))
                V.tensor_tensor(hot, lg, each(rs[:, 0, :]), ALU.is_equal).then_inc(route.sem, 1)
                dve.wait_ge(route.sem, route.at(g, 3))
                V.tensor_tensor(hot, hot, e_rank[:, :, :], ALU.mult).then_inc(route.sem, 1)
                dve.wait_ge(route.sem, route.at(g, 4))
                V.tensor_reduce(rs[:, 7, :], hot, AX.X, ALU.max).then_inc(route.sem, 1)
                dve.wait_ge(route.sem, route.at(g, 5))
                V.tensor_tensor(first, hot, each(rs[:, 7, :]), ALU.is_equal).then_inc(route.sem, 1)
                dve.wait_ge(route.sem, route.at(g, 6))
                V.scalar_tensor_tensor(out=rest, in0=first, scalar=-3.0e38, in1=lg, op0=ALU.mult, op1=ALU.add).then_inc(route.sem, 1)
                dve.wait_ge(route.sem, route.at(g, 7))
                V.tensor_reduce(rs[:, 1, :], rest, AX.X, ALU.max).then_inc(route.sem, 1)
                dve.wait_ge(route.sem, route.at(g, 8))
                V.tensor_tensor(hot, rest, each(rs[:, 1, :]), ALU.is_equal).then_inc(route.sem, 1)
                dve.wait_ge(route.sem, route.at(g, 9))
                V.tensor_tensor(hot, hot, e_rank[:, :, :], ALU.mult).then_inc(route.sem, 1)
                dve.wait_ge(route.sem, route.at(g, 10))
                V.tensor_reduce(rs[:, 7, :], hot, AX.X, ALU.max).then_inc(route.sem, 1)
                dve.wait_ge(route.sem, route.at(g, 11))
                V.tensor_tensor(second, hot, each(rs[:, 7, :]), ALU.is_equal).then_inc(route.sem, 1)
                dve.wait_ge(route.sem, route.at(g, 12))
                V.tensor_tensor(rs[:, 3, :], rs[:, 1, :], rs[:, 0, :], ALU.subtract).then_inc(route.sem, 1)
                dve.wait_ge(route.sem, route.at(g, 13))
                dve.wait_ge(e_ready.sem, e_ready.at(g, 1))
                V.tensor_scalar(rs[:, 5, :], rs[:, 4, :], 1.0, None, ALU.add).then_inc(route.sem, 1)
                dve.wait_ge(route.sem, route.at(g, 14))
                V.reciprocal(rs[:, 5, :], rs[:, 5, :]).then_inc(route.sem, 1)
                dve.wait_ge(route.sem, route.at(g, 15))
                V.tensor_tensor(rs[:, 6, :], rs[:, 4, :], rs[:, 5, :], ALU.mult).then_inc(route.sem, 1)
                dve.wait_ge(route.sem, route.at(g, 16))
                V.tensor_tensor(first, first, each(rs[:, 5, :]), ALU.mult).then_inc(route.sem, 1)
                dve.wait_ge(route.sem, route.at(g, 17))
                V.tensor_tensor(second, second, each(rs[:, 6, :]), ALU.mult).then_inc(route.sem, 1)
                dve.wait_ge(route.sem, route.at(g, 18))
                V.tensor_tensor(lg, first, second, ALU.add).then_inc(route.sem, 1)
                dve.wait_ge(route.sem, route.at(g, 19))
                gates = lg.rearrange("p (k a) e -> p k (a e)", a=2)
                V.tensor_copy(g3[:, :, 0, :], gates).then_inc(route.sem, 1)
                dve.wait_ge(route.sem, route.at(g, 20))
                V.tensor_tensor(gates, gates, g3[:, :, 0, :], ALU.subtract).then_inc(route.sem, 1)
                dve.wait_ge(route.sem, route.at(g, 21))
                V.tensor_copy(g3[:, :, 1, :], gates).then_inc(route.sem, 1)
                dve.wait_ge(route.sem, route.at(g, 22))
                V.tensor_tensor(g3[:, :, 2, :], gates, g3[:, :, 1, :], ALU.subtract).then_inc(route.sem, 1)
                dve.wait_ge(route.sem, route.at(g, 23))

            def gate(g, e):
                dve.wait_ge(gate_done.sem, gate_done.at(g, e + 1))
                dve.wait_ge(y_done.sem, y_done.at(g, max(e - 1, 0)))
                V.tensor_tensor(t_g[:, e % 2, :], t_t[:, :, :].rearrange("p k w -> p (k w)"),
                                            B_G[e % 2][:, :], ALU.mult).then_inc(tg_ready.sem, 1)

            def slot(front, back):
                def f(step, *args):
                    if front:
                        step(front[0], *args)

                def k(step, *args):
                    if back:
                        step(back[0], *args)

                k(token_mean)
                f(spread_values, 0)
                f(spread_values, 1)
                k(token_variance)
                f(bias_and_max, 0)
                f(bias_and_max, 1)
                f(bias_and_max, 2)
                f(bias_and_max, 3)
                k(routing)
                f(normalise, 0)
                k(gate, 0)
                k(gate, 1)
                f(normalise, 1)
                k(gate, 2)
                f(normalise, 2)
                k(gate, 3)
                f(normalise, 3)
                k(gate, 4)
                k(gate, 5)
                k(gate, 6)
                f(add_input, *(front or (0, 0))[1:])
                k(gate, 7)

            slots(dve, slot, phase_a)

        @block.gpsimd
        def _(pool):
            G = nc.gpsimd
            G.memset(mhalf[:, :], -0.5).then_inc(set_pool.sem, 1)
            pool.wait_ge(set_pool.sem, 1)
            G.memset(q_bd[:, :, :], 0.0).then_inc(set_pool.sem, 1)
            pool.wait_ge(set_pool.sem, 2)
            G.memset(o_t[C:C + 1, :, :], 1.0).then_inc(set_pool.sem, 1)

            def phase_a(b):
                pool.wait_ge(stat.sem, stat.at(b, 6))
                G.tensor_tensor(st[:, 5, :], st[:, 4, :], mhalf[:, :], ALU.pow).then_inc(rstd_ready.sem, 1)
                pool.wait_ge(mr_ready.sem, mr_ready.at(b, 1))

            def normalise_input(g, s):
                def over_c(v):
                    return v.unsqueeze(1).broadcast_to([P, 4, H])

                pool.wait_ge(qkv_done.sem, qkv_done.at(g))
                G.tensor_tensor(xn[:, :, :], xt[:, bass.ds(s * 4, 4), :], over_c(st[:, 5, :]), ALU.mult).then_inc(xn_ready.sem, 1)
                pool.wait_ge(xn_ready.sem, xn_ready.at(g, 1))
                G.tensor_tensor(xn[:, :, :], xn[:, :, :], over_c(st[:, 0, :]), ALU.subtract).then_inc(xn_ready.sem, 1)

            def shift(g, i):
                pool.wait_ge(mx_ready.sem, mx_ready.at(g, i + 1))
                sc = prob[:, i].rearrange("p n h k -> p (n h) k")
                G.tensor_tensor(sc, sc, mx[:, i, :].unsqueeze(2).broadcast_to([P, 2 * HEADS, NTOK]),
                                             ALU.subtract).then_inc(s_shifted.sem, 1)

            def normalise_tokens(g):
                def over_c(v):
                    return v.unsqueeze(2).broadcast_to([P, ROWS, C])

                pool.wait_ge(lsum.sem, lsum.at(g, 2))
                G.tensor_tensor(xc[:, :, :], x2[:, :, :], over_c(ln[:, 1, :]), ALU.subtract).then_inc(xc_ready.sem, 1)
                pool.wait_ge(lvar.sem, lvar.at(g, 2))
                G.tensor_tensor(ln[:, 3, :], ln[:, 2, :], mhalf[:, 0:ROWS], ALU.pow).then_inc(lrstd.sem, 1)
                pool.wait_ge(lrstd.sem, lrstd.at(g, 1))
                G.tensor_tensor(t_n[:, :, :], xc[:, :, :], over_c(ln[:, 3, :]), ALU.mult).then_inc(t_ready.sem, 1)

            def slot(front, back):
                if front:
                    normalise_input(*front)
                if back:
                    normalise_tokens(back[0])
                if front:
                    for i in range(UNITS):
                        shift(front[0], i)

            slots(pool, slot, phase_a)


SET_DVE = 10
SET_POOL = 3
ROUTE_GAP = 13


def rel_index():
    m = np.arange(NTOK)
    r, c = m // 4 % 8, 2 * (m % 4) + m // 32
    return (m[:, None] // WS - r[None, :] + WS - 1) * (2 * WS - 1) + m[:, None] % WS - c[None, :] + WS - 1


_SHAPE = (BATCH, C, H, W)


def kernel(x, L0_conv_Wq, L0_conv_bq, L0_conv_Wkv, L0_conv_bkv, L0_conv_rel_bias, L0_conv_Wproj, L0_conv_bproj,
           L0_ffn_router_w, L0_ffn_router_b, L0_ffn_expert_w, L0_ffn_expert_b):
    import concourse.bacc as _bacc
    from concourse.bass_utils import run_bass_kernel_spmd as _run

    f = np.float32
    a = {k: np.asarray(v) for k, v in dict(
        x=x, wq=L0_conv_Wq, bq=L0_conv_bq, wkv=L0_conv_Wkv, bkv=L0_conv_bkv, rel=L0_conv_rel_bias, wp=L0_conv_Wproj,
        bp=L0_conv_bproj, rw=L0_ffn_router_w, rb=L0_ffn_router_b, ew=L0_ffn_expert_w, eb=L0_ffn_expert_b).items()}
    wqkv = np.concatenate([a["wq"][:, None], a["wkv"].reshape(C, 2, C)], 1)
    qkvb = np.concatenate([a["bq"][:, None], a["bkv"].reshape(2, C).T], 1)
    zero = np.zeros_like(wqkv)
    wexp = np.zeros((P, EXPERTS, P), f)
    wrout = np.zeros((P, 2 * EXPERTS), f)
    for g in range(2):
        wexp[C * g:C * g + C, :, C * g:C * g + C] = a["ew"].transpose(1, 0, 2)
        wrout[C * g:C * g + C, EXPERTS * g:EXPERTS * g + EXPERTS] = a["rw"]
    bexp = np.zeros((PARTS, 2, EXPERTS, 2, C), f)
    sel = np.zeros((PARTS, 2, EXPERTS, EXPERTS, 2, C), f)
    for g in range(2):
        bexp[:, g, :, g, :] = a["eb"]
        for e in range(EXPERTS):
            sel[:, g, e, e, g, :] = 1.0
    kmask = np.zeros((2, HEADS, DH, HEADS), f)
    kbias = np.zeros((2, HEADS, DH, HEADS), f)
    for h in range(HEADS):
        kmask[:, h, :, h] = 1.0
        kbias[:, h, :, h] = a["bkv"][:C].reshape(HEADS, DH)[h]
    relb = a["rel"][rel_index()].transpose(0, 2, 1).reshape(NTOK, HEADS * NTOK)
    arrays = {
        "x": a["x"],
        "wqkv": np.stack([np.concatenate([wqkv, zero]), np.concatenate([zero, wqkv])], 1),
        "qkvb": np.concatenate([qkvb, qkvb]),
        "kmask": kmask.reshape(P, HEADS),
        "kbias": kbias.reshape(P, HEADS),
        "wproj": np.concatenate([a["wp"], a["bp"][None]]),
        "wrout": wrout,
        "brout": np.broadcast_to(a["rb"], (P, ROWS, EXPERTS)),
        "wexp": wexp,
        "bexp": bexp.reshape(GROWS, P),
        "relb": np.concatenate([relb, relb]),
        "ident": np.eye(P, dtype=f),
        "sel": sel.reshape(GROWS, EXPERTS, P),
        "rank": np.broadcast_to(np.arange(EXPERTS, 0, -1, dtype=f), (P, ROWS, EXPERTS)),
    }
    arrays = {k: np.ascontiguousarray(v) for k, v in arrays.items()}
    nc = _bacc.Bacc("TRN2", target_bir_lowering=False, num_devices=1)
    args = [nc.dram_tensor(f"in_{k}", v.shape, F32, kind="ExternalInput").ap() for k, v in arrays.items()]
    out = nc.dram_tensor("out_y", _SHAPE, F32, kind="ExternalOutput").ap()
    build(nc, *args, out)
    r = _run(nc, [{f"in_{k}": v for k, v in arrays.items()}], core_ids=[0])
    return r.results[0]["out_y"]
```

```python
from contextlib import ExitStack

import numpy as np

import concourse.bass as bass
from concourse import mybir

F32 = mybir.dt.float32
BF16 = mybir.dt.bfloat16
ALU = mybir.AluOpType
ACT = mybir.ActivationFunctionType
AX = mybir.AxisListType

BATCH, C, H, W = 4, 64, 128, 128
P = 128
HEADS, DH = 4, 16
WS = 8
NTOK = WS * WS
STRIPS = C // 4
PAIRS = 8
UNITS = PAIRS // 2
BANK = 512
EXPERTS = 8
MIXES = EXPERTS
ON_POOL = (3, 7)
ON_DVE = tuple(u for u in range(MIXES) if u not in ON_POOL)
TG = 4
ROWS = 8
GROUPS = C // 4
RING = 4
PVW = 96
PARTS = 3
GROWS = PARTS * 2 * EXPERTS
LN_C_EPS, LN_T_EPS = 1e-6, 1e-5


class Sem:

    def __init__(self, sem, per=1, primed=0):
        self.sem, self.per, self.primed = sem, per, primed

    def at(self, n, k=0):
        return n * self.per + (k + self.primed)


def build(nc, x, wqkv, qkvb, kmask, kbias, wproj, wrout, brout, wexp, bexp, relb, ident, sel, rank, out):
    ctx = ExitStack()
    with ctx:
        def sb(name, shape, dt=F32):
            return ctx.enter_context(nc.sbuf_tensor(name, shape, dt))

        def sem(name, per=1, primed=0):
            s = Sem(ctx.enter_context(nc.semaphore(name)), per, primed)
            primed_sems.extend([s] * primed)
            return s

        primed_sems = []

        w_qkv = sb("w_qkv", [P, 2, 3, C])
        b_qkv = sb("b_qkv", [P, 3])
        q_bias = sb("q_bias", [P, 1])
        k_mask = sb("k_mask", [P, HEADS])
        k_bias = sb("k_bias", [P, HEADS])
        w_proj = sb("w_proj", [C + 1, C])
        w_rout = sb("w_rout", [C, EXPERTS])
        b_rout = sb("b_rout", [P, ROWS, EXPERTS])
        w_exp = sb("w_exp", [P, MIXES // 2, C])
        b_exp = sb("b_exp", [GROWS, P])
        b_exp_part = sb("b_exp_part", [GROWS, PARTS, P], BF16)
        rel = sb("rel", [P, HEADS * NTOK])
        idn = sb("idn", [P, P])
        idn16 = sb("idn16", [P, P], BF16)
        gate_sel = sb("gate_sel", [GROWS, MIXES, P])
        gate_sel16 = sb("gate_sel16", [GROWS, MIXES, P], BF16)
        e_rank = sb("e_rank", [P, ROWS, EXPERTS])
        mhalf = sb("mhalf", [P, H])

        x_in = sb("x_in", [P, RING, 4, W])
        xt = sb("xt", [P, 2 * C, H])
        x_sq = sb("x_sq", [P, 2, 4, H])
        sums = sb("sums", [P, H, GROUPS])
        sums2 = sb("sums2", [P, H, GROUPS])
        st = sb("st", [P, 5, H])
        rstd = sb("rstd", [P, 2, H])
        m_rstd = sb("m_rstd", [P, 2, H])

        xn = sb("xn", [P, 4, H])
        q_bd = sb("q_bd", [P, 2, PAIRS, 2 * NTOK])
        k_m = sb("k_m", [P, 2, PAIRS, HEADS, NTOK])
        v_t = sb("v_t", [P, PAIRS + 1, NTOK])
        v_bd = sb("v_bd", [P, 2, PAIRS, 2, PVW])
        prob = sb("prob", [P, UNITS, 2, HEADS, NTOK])
        mx = sb("mx", [P, UNITS, 2 * HEADS])
        prob_t = sb("prob_t", [P, 2, 2, 2, P])
        r_sum = sb("r_sum", [P, UNITS, 4, 2])
        o_n = sb("o_n", [P, PAIRS, C])
        o_t = sb("o_t", [C + 1, ROWS, W])
        x2 = sb("x2", [P, 2, ROWS, C])

        ln = sb("ln", [P, 4, ROWS])
        xc = sb("xc", [P, ROWS, C])
        xc2 = sb("xc2", [P, ROWS, C])
        t_n = sb("t_n", [P, ROWS, C])
        t_t = sb("t_t", [P, 2, 2, BANK])
        rt = sb("rt", [P, 8, ROWS, EXPERTS])
        rs = sb("rs", [P, 8, ROWS])
        g3 = sb("g3", [P, 4, PARTS, 2 * EXPERTS], BF16)
        g_t = sb("g_t", [GROWS, BANK], BF16)
        t_g = sb("t_g", [P, TG, BANK])
        g_copy = sb("g_copy", [P, 2, BANK])
        y_out = sb("y_out", [P, 4, W])

        bank = [ctx.enter_context(nc.psum_tensor(f"bank{i}", [P, BANK], F32)) for i in range(8)]
        B_S = bank[0:2]
        B_T = bank[2:4]
        B_M = bank[4]
        B_P = bank[5]
        B_G = bank[6]
        B_Y = bank[7]

        loads = ctx.enter_context(nc.semaphore("weights_loaded"))
        x_loaded = [Sem(ctx.enter_context(nc.semaphore(f"x_loaded{r}"))) for r in range(RING)]
        passed = ctx.enter_context(nc.semaphore("passed"))
        stored = ctx.enter_context(nc.semaphore("stored"))
        set_pool = sem("set_pool")
        set_dve = sem("set_dve")
        set_act = sem("set_act")
        x_turned = sem("x_turned")
        xt_ready = sem("xt_ready", primed=1)
        sq_ready = sem("sq_ready")
        part_sums = sem("part_sums", 2, primed=1)
        stat = sem("stat", 6)
        rstd_ready = sem("rstd_ready")
        mr_ready = sem("mr_ready")

        xn_ready = sem("xn_ready", 2)
        qkv_done = sem("qkv_done", 3, primed=1)
        q_ready = sem("q_ready", 4)
        k_ready = sem("k_ready", 4)
        v_ready = sem("v_ready", 2)
        vrow_done = sem("vrow_done", 2)
        vbd_ready = sem("vbd_ready", 10, primed=1)
        s_done = sem("s_done", UNITS)
        s_biased = sem("s_biased", UNITS, primed=1)
        mx_ready = sem("mx_ready", UNITS)
        s_shifted = sem("s_shifted", UNITS)
        p_ready = sem("p_ready", UNITS)
        pt_done = sem("pt_done", UNITS)
        pt_ready = sem("pt_ready", UNITS)
        pv_done = sem("pv_done", UNITS, primed=1)
        rsum_ready = sem("rsum_ready", UNITS)
        on_ready = sem("on_ready", 2 * UNITS)
        ot_done = sem("ot_done", 2)
        ot_ready = sem("ot_ready", 4, primed=1)
        proj_done = sem("proj_done")
        x2_ready = sem("x2_ready", primed=1)

        lsum = sem("lsum", 2)
        xc_ready = sem("xc_ready")
        xc2_ready = sem("xc2_ready")
        lvar = sem("lvar", 2)
        lrstd = sem("lrstd")
        t_ready = sem("t_ready")
        tt_done = sem("tt_done")
        tt_ready = sem("tt_ready", 4)
        logits_done = sem("logits_done")
        route = sem("route", 23)
        e_ready = sem("e_ready")
        gt_done = sem("gt_done")
        gt_ready = sem("gt_ready")
        gate_done = sem("gate_done", MIXES)
        g_copied = sem("g_copied", len(ON_POOL))
        tg_dve = sem("tg_dve", MIXES - len(ON_POOL), primed=1)
        tg_pool = sem("tg_pool", len(ON_POOL))
        y_done = sem("y_done", MIXES, primed=1)
        y_ready = sem("y_ready", primed=1)

        consts = [(w_qkv, wqkv), (b_qkv, qkvb), (k_mask, kmask), (k_bias, kbias), (w_proj, wproj), (w_rout, wrout),
                  (b_rout, brout), (w_exp, wexp), (b_exp, bexp), (rel, relb), (idn, ident),
                  (gate_sel, sel), (e_rank, rank)]
        ALL_LOADED = 16 * len(consts)

        block = ctx.enter_context(nc.Block())

        def turned(ap):
            return ap.rearrange("p (a v l) -> p v a l", v=PAIRS, l=4)

        def pipeline(eng, slot, take, statistics):
            all_on = ("project", "attend", "route", "mix")
            with eng.Fori(0, 4) as t:
                for r in range(2):
                    take(0, t, r)
            statistics(0)
            slot(-1, 1, None, all_on[:1])
            slot(0, 0, None, all_on[:2])
            slot(1, 1, None, all_on[:3])
            with eng.Fori(0, BATCH - 1) as b:
                with eng.Fori(0, 4) as t:
                    for r in range(2):
                        slot(b * STRIPS + t * 2 + (2 + r), r, (b + 1, t), all_on)
                statistics(b + 1)
                with eng.Fori(4, 8) as t:
                    for r in range(2):
                        slot(b * STRIPS + t * 2 + (2 + r), r, None, all_on)
            with eng.Fori(0, 6) as t:
                for r in range(2):
                    slot(t * 2 + (STRIPS * (BATCH - 1) + 2 + r), r, None, all_on)
            last = STRIPS * BATCH - 1
            slot(last - 1, 0, None, all_on)
            slot(last, 1, None, all_on[1:])
            slot(last + 1, 0, None, all_on[2:])
            slot(last + 2, 1, None, all_on[3:])

        @block.sync
        def _(sp):
            for s in primed_sems:
                sp.sem_inc(s.sem, 1)
            sp.sem_inc(stored, 1)
            xg = x.rearrange("b (q c) h w -> (b q) h c w", c=4)
            for r in range(RING):
                sp.dma_start(x_in[:, r], xg[r]).then_inc(x_loaded[r].sem, 16)
            for dst, src in consts:
                sp.dma_start(dst[tuple(slice(None) for _ in dst.shape)], src).then_inc(loads, 16)
            with sp.Fori(0, BATCH * GROUPS // RING - 1) as t:
                for r in range(RING):
                    sp.wait_ge(x_turned.sem, x_turned.at(t * RING, r + 1))
                    sp.dma_start(x_in[:, r], xg[bass.ds(t * RING + RING + r, 1)].rearrange("o h c w -> h (o c) w")
                                 ).then_inc(x_loaded[r].sem, 16)

        @block.tensor
        def _(pe):
            mm, tr = nc.tensor.matmul, nc.tensor.transpose
            pe.wait_ge(loads, ALL_LOADED)
            pe.wait_ge(set_dve.sem, SET_DVE)
            pe.wait_ge(set_pool.sem, SET_POOL)

            def take(batch, t, r):
                for m in range(2):
                    n = 2 * r + m
                    pe.wait_ge(x_loaded[n].sem, (batch * (GROUPS // RING) + t + 1) * 16)
                    if isinstance(batch, int):
                        pe.wait_ge(xt_ready.sem, xt_ready.at(t * RING, max(n - 1, 0)))
                    for c in range(4):
                        last = tr(B_T[m][:, c * H:(c + 1) * H], x_in[:, n, c, :], idn[:, :])
                    last.then_inc(x_turned.sem, 1)

            def project(g, i, dst):
                if i == 1:
                    pe.wait_ge(xn_ready.sem, xn_ready.at(g, 2))
                    if isinstance(g, int) and g == 1:
                        pe.wait_ge(vbd_ready.sem, vbd_ready.at(1))
                    elif not (isinstance(g, int) and g == 0):
                        pe.wait_ge(x2_ready.sem, x2_ready.at(g - 1))
                elif i == 0:
                    pe.wait_ge(vbd_ready.sem, vbd_ready.at(g))
                elif i == 2:
                    pe.wait_ge(q_ready.sem, q_ready.at(g, 4))
                for half in range(2):
                    for ab in range(2):
                        src = xn[:, :, :].rearrange("p c (hh ab l) -> p (c hh) ab l", ab=2, l=32)[:, :, ab, :]
                        last = mm(dst[C * ab:C * ab + C, 256 * half:256 * half + 256], w_qkv[:, half, i, :], src,
                                  start=True, stop=True, skip_group_check=True)
                last.then_inc(qkv_done.sem, 1)

            def turn_values(g, u, dst):
                pe.wait_ge(v_ready.sem, v_ready.at(g, 2))
                if u == 0:
                    pe.wait_ge(k_ready.sem, k_ready.at(g, 4))
                for n in range(4):
                    v = 4 * u + n
                    last = tr(dst[:, n * P:(n + 1) * P], v_t[:, v:v + 2, :].rearrange("p v t -> p (v t)"), idn[:, :])
                last.then_inc(vrow_done.sem, 1)

            def scores(g, p, i):
                if i == 0:
                    pe.wait_ge(q_ready.sem, q_ready.at(g, 4))
                    pe.wait_ge(k_ready.sem, k_ready.at(g, 4))
                pe.wait_ge(s_biased.sem, s_biased.at(g, max(i - 1, 0)))
                for n in range(2):
                    v = 2 * i + n
                    last = mm(B_S[i % 2][:, n * 256:(n + 1) * 256], q_bd[:, p, v, :],
                              k_m[:, p, v, :, :].rearrange("p h k -> p (h k)"), start=True, stop=True,
                              skip_group_check=True)
                last.then_inc(s_done.sem, 1)

            def turn_probs(g, i):
                pe.wait_ge(p_ready.sem, p_ready.at(g, i + 1))
                if i >= 2:
                    pe.wait_ge(pt_ready.sem, pt_ready.at(g, i - 1))
                for n in range(2):
                    for hp in range(2):
                        at = (2 * n + hp) * P
                        last = tr(B_T[i % 2][:, at:at + P],
                                  prob[:, i, n, 2 * hp:2 * hp + 2, :].rearrange("p h k -> p (h k)"), idn[:, :])
                last.then_inc(pt_done.sem, 1)

            def values(g, p, i, projecting):
                pe.wait_ge(pt_ready.sem, pt_ready.at(g, i + 1))
                if i:
                    pe.wait_ge(on_ready.sem, on_ready.at(g, 2 * i))
                elif projecting:
                    pe.wait_ge(vbd_ready.sem, vbd_ready.at(g + 1, 4))
                else:
                    pe.wait_ge(x2_ready.sem, x2_ready.at(g))
                for n in range(2):
                    for hp in range(2):
                        at = (2 * n + hp) * PVW
                        last = mm(B_M[:, at:at + PVW], prob_t[:, i % 2, n, hp, :], v_bd[:, p, 2 * i + n, hp, :],
                                  start=True, stop=True, skip_group_check=True)
                last.then_inc(pv_done.sem, 1)

            def turn_outputs(g, u):
                pe.wait_ge(on_ready.sem, on_ready.at(g, 4 * u + 4))
                pe.wait_ge(pt_ready.sem, pt_ready.at(g, 3 + u))
                pe.sem_inc(passed, 1)
                for n in range(4):
                    last = tr(B_T[u][0:C, n * P:(n + 1) * P], o_n[:, 4 * u + n, :], idn[:, :])
                last.then_inc(ot_done.sem, 1)

            def project_out(g):
                pe.wait_ge(ot_ready.sem, ot_ready.at(g, 4))
                pe.wait_ge(on_ready.sem, on_ready.at(g, 8))
                for r in range(ROWS):
                    at = (r % 4 * 2 + r // 4) * C
                    last = mm(B_M[:, at:at + C], o_t[:, r, :], w_proj[:, :], start=True, stop=True,
                              skip_group_check=True)
                last.then_inc(proj_done.sem, 1)

            def turn_tokens(g, projecting):
                pe.wait_ge(t_ready.sem, t_ready.at(g, 1))
                if projecting:
                    pe.wait_ge(vbd_ready.sem, vbd_ready.at(g + 2, 10))
                else:
                    pe.wait_ge(gt_ready.sem, gt_ready.at(g - 1, 1))
                for k in range(4):
                    src = t_n[:, 2 * k:2 * k + 2, :].rearrange("p a c -> p (a c)")
                    last = tr(B_P[:, k * P:(k + 1) * P], src, idn[:, :])
                last.then_inc(tt_done.sem, 1)

            def logits(g, p):
                pe.wait_ge(tt_ready.sem, tt_ready.at(g, 4))
                for k in range(4):
                    for a in range(2):
                        at = (2 * k + a) * EXPERTS
                        last = mm(B_P[:, at:at + EXPERTS], t_t[0:C, p, a, k * P:(k + 1) * P], w_rout[:, :],
                                  start=True, stop=True, skip_group_check=True)
                last.then_inc(logits_done.sem, 1)

            def turn_gates(g):
                pe.wait_ge(route.sem, route.at(g, route.per))
                pe.sem_inc(passed, 1)
                gt16 = B_P[:, :].bitcast(BF16)
                for k in range(4):
                    last = tr(gt16[0:GROWS, k * P:(k + 1) * P], g3[:, k].rearrange("p a e -> p (a e)"), idn16[:, :])
                last.then_inc(gt_done.sem, 1)

            def start_sum(g, p):
                pe.wait_ge(y_ready.sem, y_ready.at(g))
                for k in range(4):
                    src = x2[:, p, 2 * k:2 * k + 2, :].rearrange("p a c -> p (a c)")
                    mm(B_Y[:, k * P:(k + 1) * P], src, idn[:, :], is_transpose=True, start=(k == 0), stop=False,
                       skip_group_check=True)
                pe.wait_ge(gt_ready.sem, gt_ready.at(g, 1))
                for part in range(PARTS):
                    mm(B_Y[:, :], b_exp_part[:, part, :], g_t[:, :], start=False, stop=False, skip_group_check=True)

            def gates(g, u):
                if u and u - 1 in ON_POOL:
                    pe.wait_ge(g_copied.sem, g_copied.at(g, ON_POOL.index(u - 1) + 1))
                elif u:
                    pe.wait_ge(tg_dve.sem, tg_dve.at(g, ON_DVE.index(u - 1) + 1))
                mm(B_G[:, :], gate_sel16[:, u, :], g_t[:, :], start=True, stop=True).then_inc(gate_done.sem, 1)

            def expert(g, u):
                if u in ON_POOL:
                    pe.wait_ge(tg_pool.sem, tg_pool.at(g, ON_POOL.index(u) + 1))
                else:
                    pe.wait_ge(tg_dve.sem, tg_dve.at(g, ON_DVE.index(u) + 1))
                a = u % 2
                mm(B_Y[C * a:C * a + C, :], w_exp[:, u // 2, :], t_g[:, u % TG, :], start=False,
                   stop=(u // 2 == MIXES // 2 - 1), skip_group_check=True).then_inc(y_done.sem, 1)

            def slot(j, p, group, on):
                P_, F_, R_, M_ = ("project" in on, "attend" in on, "route" in on, "mix" in on)
                if group:
                    take(*group, p)
                if F_:
                    scores(j, p, 0)
                    scores(j, p, 1)
                if M_:
                    turn_gates(j - 2)
                if P_:
                    project(j + 1, 1, B_M)
                if M_:
                    start_sum(j - 2, p)
                    gates(j - 2, 0)
                if P_:
                    if M_:
                        pe.wait_ge(gt_ready.sem, gt_ready.at(j - 2, 1))
                    project(j + 1, 0, B_P)
                if M_:
                    gates(j - 2, 1)
                if F_:
                    scores(j, p, 2)
                if P_:
                    project(j + 1, 2, B_P)
                if F_:
                    turn_probs(j, 0)
                    scores(j, p, 3)
                if M_:
                    gates(j - 2, 2)
                    expert(j - 2, 0)
                    expert(j - 2, 1)
                if P_:
                    turn_values(j + 1, 0, B_M)
                    turn_values(j + 1, 1, B_P)
                if F_:
                    turn_probs(j, 1)
                if M_:
                    gates(j - 2, 3)
                if F_:
                    values(j, p, 0, P_)
                if R_:
                    turn_tokens(j - 1, P_)
                if M_:
                    gates(j - 2, 4)
                    expert(j - 2, 2)
                if F_:
                    turn_probs(j, 2)
                    values(j, p, 1, P_)
                if M_:
                    gates(j - 2, 5)
                    expert(j - 2, 3)
                if F_:
                    turn_probs(j, 3)
                    values(j, p, 2, P_)
                if R_:
                    logits(j - 1, 1 - p)
                if M_:
                    gates(j - 2, 6)
                    expert(j - 2, 4)
                    expert(j - 2, 5)
                if F_:
                    turn_outputs(j, 0)
                    values(j, p, 3, P_)
                if M_:
                    gates(j - 2, 7)
                if F_:
                    turn_outputs(j, 1)
                if M_:
                    expert(j - 2, 6)
                if F_:
                    project_out(j)
                if M_:
                    expert(j - 2, 7)

            pipeline(pe, slot, take, lambda batch: None)

        @block.scalar
        def _(act):
            A = nc.scalar.activation
            act.wait_ge(loads, ALL_LOADED)
            A(q_bias[:, :], b_qkv[:, 0:1], ACT.Copy, scale=float(DH) ** -0.5).then_inc(set_act.sem, 1)
            act.wait_ge(set_act.sem, 1)
            act.wait_ge(set_pool.sem, SET_POOL)

            def take(batch, t, r):
                n = batch * GROUPS + t * RING
                plane = (n % (2 * GROUPS)) * 4
                for m in range(2):
                    dst = xt[:, bass.ds(plane + (2 * r + m) * 4, 4), :]
                    act.wait_ge(x_turned.sem, x_turned.at(n, 2 * r + m + 1))
                    act.sem_inc(passed, 1)
                    A(dst, B_T[m][:, :].rearrange("p (c h) -> p c h", c=4), ACT.Copy).then_inc(xt_ready.sem, 1)
                for m in range(2):
                    act.wait_ge(xt_ready.sem, xt_ready.at(n, 2 * r + m + 1))
                    act.wait_ge(part_sums.sem, part_sums.at(n + 2 * r))
                    act.sem_inc(passed, 1)
                    A(x_sq[:, m], xt[:, bass.ds(plane + (2 * r + m) * 4, 4), :], ACT.Square).then_inc(sq_ready.sem, 1)

            def copy_q(g, p):
                act.wait_ge(qkv_done.sem, qkv_done.at(g, 2))
                for ab in range(2):
                    rows = slice(C * ab, C * ab + C)
                    for half in range(2):
                        A(q_bd[rows, p, :, ab * NTOK:(ab + 1) * NTOK].rearrange("p v (r l a) -> p v r l a", a=2, l=4)[
                            :, :, :, :, half],
                          turned(B_P[rows, 256 * half:256 * half + 256]), ACT.Identity, bias=q_bias[rows, :],
                          scale=float(DH) ** -0.5).then_inc(q_ready.sem, 1)

            def copy_k(g, p):
                act.wait_ge(qkv_done.sem, qkv_done.at(g, 1))
                for h in range(HEADS):
                    A(k_m[:, p, :, h, :].rearrange("p v (a l) -> p v a l", l=4), turned(B_M[:, :]), ACT.Identity,
                      bias=k_bias[:, h:h + 1], scale=k_mask[:, h:h + 1]).then_inc(k_ready.sem, 1)

            def copy_v(g):
                act.wait_ge(qkv_done.sem, qkv_done.at(g, 3))
                A(v_t[:, 0:PAIRS, :].rearrange("p v (a l) -> p v a l", l=4), turned(B_P[:, :]), ACT.Identity,
                  bias=b_qkv[:, 2:3]).then_inc(v_ready.sem, 1)
                A(v_t[:, PAIRS, :].rearrange("p (a l) -> p a l", l=4), turned(B_P[:, :])[:, 0], ACT.Identity,
                  bias=b_qkv[:, 2:3]).then_inc(v_ready.sem, 1)

            def exps(g, i):
                act.wait_ge(s_shifted.sem, s_shifted.at(g, i + 1))
                A(prob[:, i], prob[:, i], ACT.Exp).then_inc(p_ready.sem, 1)

            def copy_probs(g, i):
                act.wait_ge(pt_done.sem, pt_done.at(g, i + 1))
                act.wait_ge(pv_done.sem, pv_done.at(g, max(i - 1, 0)))
                A(prob_t[:, i % 2].rearrange("p n h q -> p (n h q)"), B_T[i % 2][:, :],
                  ACT.Copy).then_inc(pt_ready.sem, 1)

            def copy_outputs(g, u):
                act.wait_ge(ot_done.sem, ot_done.at(g, u + 1))
                for ab in range(2):
                    at = (PAIRS * ab + 4 * u) * WS
                    A(o_t[0:C, :, at:at + 4 * WS].rearrange("c r (v s) -> c v r s", s=WS),
                      B_T[u][0:C, :].rearrange("c (v ab r s) -> c ab v r s", v=4, ab=2, s=WS)[:, ab],
                      ACT.Copy).then_inc(ot_ready.sem, 1)

            def square(g):
                act.wait_ge(xc_ready.sem, xc_ready.at(g, 1))
                A(xc2[:, :, :], xc[:, :, :], ACT.Square).then_inc(xc2_ready.sem, 1)

            def copy_tokens(g, p):
                act.wait_ge(tt_done.sem, tt_done.at(g, 1))
                for a in range(2):
                    for copy in range(2):
                        A(t_t[C * copy:C * copy + C, p, a, :], B_P[C * a:C * a + C, :],
                          ACT.Copy).then_inc(tt_ready.sem, 1)

            def gate_exp(g):
                act.wait_ge(route.sem, route.at(g, ROUTE_GAP))
                A(rs[:, 4, :], rs[:, 3, :], ACT.Exp).then_inc(e_ready.sem, 1)

            def copy_turned_gates(g):
                act.wait_ge(gt_done.sem, gt_done.at(g, 1))
                A(g_t[:, :], B_P[:, :].bitcast(BF16)[0:GROWS, 0:BANK], ACT.Copy).then_inc(gt_ready.sem, 1)

            def copy_gates(g, u):
                act.wait_ge(gate_done.sem, gate_done.at(g, u + 1))
                A(g_copy[:, ON_POOL.index(u) % 2, :], B_G[:, :], ACT.Copy).then_inc(g_copied.sem, 1)

            def store(g):
                act.wait_ge(y_done.sem, y_done.at(g, MIXES))
                act.wait_ge(stored, g * 32 + 1)
                A(y_out[:, :, :].rearrange("p k w -> p (k w)"), B_Y[:, :], ACT.Copy).then_inc(y_ready.sem, 1)
                act.wait_ge(y_ready.sem, y_ready.at(g, 1))
                for a in range(2):
                    dst = out[bass.ds(g // STRIPS, 1), :, bass.ds((g % STRIPS) * ROWS + 4 * a, 4), :]
                    act.dma_start(dst.rearrange("o c k w -> (o c) k w"), y_out[C * a:C * a + C]).then_inc(stored, 16)

            def slot(j, p, group, on):
                P_, F_, R_, M_ = ("project" in on, "attend" in on, "route" in on, "mix" in on)
                if group:
                    take(*group, p)
                if M_:
                    copy_turned_gates(j - 2)
                if R_:
                    square(j - 1)
                if P_:
                    copy_k(j + 1, 1 - p)
                if F_:
                    exps(j, 0)
                if P_:
                    copy_q(j + 1, 1 - p)
                if F_:
                    exps(j, 1)
                if P_:
                    copy_v(j + 1)
                if F_:
                    copy_probs(j, 0)
                    exps(j, 2)
                if M_:
                    copy_gates(j - 2, 3)
                if F_:
                    copy_probs(j, 1)
                    exps(j, 3)
                if R_:
                    copy_tokens(j - 1, 1 - p)
                if F_:
                    copy_probs(j, 2)
                    copy_probs(j, 3)
                    copy_outputs(j, 0)
                if M_:
                    copy_gates(j - 2, 7)
                if F_:
                    copy_outputs(j, 1)
                if R_:
                    gate_exp(j - 1)
                if M_:
                    store(j - 2)

            pipeline(act, slot, take, lambda batch: None)
            act.wait_ge(stored, BATCH * STRIPS * 32 + 1)

        @block.vector
        def _(dve):
            V = nc.vector
            dve.wait_ge(loads, ALL_LOADED)
            V.memset(v_bd[:, :, :, :, :], 0.0).then_inc(set_dve.sem, 1)
            dve.wait_ge(set_dve.sem, 1)
            for j in range(2):
                V.memset(v_bd[C * j:C * j + C, :, :, :, 64 + j:65 + j], 1.0).then_inc(set_dve.sem, 1)
            V.tensor_copy(idn16[:, :], idn[:, :]).then_inc(set_dve.sem, 1)
            V.tensor_copy(gate_sel16[:, :, :], gate_sel[:, :, :]).then_inc(set_dve.sem, 1)
            V.tensor_copy(b_exp_part[:, 0, :], b_exp[:, :]).then_inc(set_dve.sem, 1)
            for part in range(1, PARTS):
                dve.wait_ge(set_dve.sem, 4 + 2 * part)
                V.tensor_tensor(b_exp[:, :], b_exp[:, :], b_exp_part[:, part - 1, :], ALU.subtract).then_inc(set_dve.sem, 1)
                dve.wait_ge(set_dve.sem, 5 + 2 * part)
                V.tensor_copy(b_exp_part[:, part, :], b_exp[:, :]).then_inc(set_dve.sem, 1)

            def take(batch, t, r):
                n = batch * GROUPS + t * RING
                plane = (n % (2 * GROUPS)) * 4
                for m in range(2):
                    q = t * RING + (2 * r + m)
                    dve.wait_ge(xt_ready.sem, xt_ready.at(n, 2 * r + m + 1))
                    V.tensor_reduce(sums[:, :, bass.ds(q, 1)].rearrange("p h o -> p (h o)"),
                                    xt[:, bass.ds(plane + (2 * r + m) * 4, 4), :].rearrange("p c h -> p h c"),
                                    AX.X, ALU.add).then_inc(part_sums.sem, 1)
                for m in range(2):
                    q = t * RING + (2 * r + m)
                    dve.wait_ge(sq_ready.sem, sq_ready.at(n, 2 * r + m + 1))
                    V.tensor_reduce(sums2[:, :, bass.ds(q, 1)].rearrange("p h o -> p (h o)"),
                                    x_sq[:, m].rearrange("p c h -> p h c"), AX.X, ALU.add).then_inc(part_sums.sem, 1)

            def statistics(batch):
                par = batch % 2
                dve.wait_ge(part_sums.sem, part_sums.at(batch * GROUPS + GROUPS))
                V.tensor_reduce(st[:, 0, :], sums[:, :, :], AX.X, ALU.add).then_inc(stat.sem, 1)
                V.tensor_reduce(st[:, 1, :], sums2[:, :, :], AX.X, ALU.add).then_inc(stat.sem, 1)
                dve.wait_ge(stat.sem, stat.at(batch, 2))
                V.tensor_scalar(st[:, 2, :], st[:, 0, :], 1.0 / C, None, ALU.mult).then_inc(stat.sem, 1)
                dve.wait_ge(stat.sem, stat.at(batch, 3))
                V.tensor_tensor(st[:, 3, :], st[:, 2, :], st[:, 2, :], ALU.mult).then_inc(stat.sem, 1)
                dve.wait_ge(stat.sem, stat.at(batch, 4))
                V.scalar_tensor_tensor(out=st[:, 4, :], in0=st[:, 1, :], scalar=1.0 / C, in1=st[:, 3, :],
                                       op0=ALU.mult, op1=ALU.subtract).then_inc(stat.sem, 1)
                dve.wait_ge(stat.sem, stat.at(batch, 5))
                V.tensor_scalar(st[:, 4, :], st[:, 4, :], 0.0, LN_C_EPS, ALU.max, ALU.add).then_inc(stat.sem, 1)

            def spread_values(g, p, u):
                dve.wait_ge(vrow_done.sem, vrow_done.at(g, u + 1))
                src = (B_M, B_P)[u]
                runs = [(0, 0, 4, 4 * u), (1, 0, 4, 1)] if u == 0 else [(0, 0, 4, 4), (1, 0, 3, 5), (1, 3, 1, 0)]
                for j, n0, count, v0 in runs:
                    rows = slice(C * j, C * j + C)
                    for hp in range(2):
                        at = (2 * hp + j) * DH
                        V.tensor_copy(
                            v_bd[rows, p, v0:v0 + count, hp, 0:64].rearrange("p v (ab c) -> p v ab c", ab=2)[
                                :, :, :, j * DH:(j + 1) * DH],
                            src[rows, :].rearrange("p (v ab c) -> p v ab c", v=4, ab=2)[
                                :, n0:n0 + count, :, at:at + DH]).then_inc(vbd_ready.sem, 1)

            def bias_and_max(g, i):
                dve.wait_ge(s_done.sem, s_done.at(g, i + 1))
                V.tensor_tensor(
                    prob[:, i].rearrange("p n h k -> p n (h k)"), B_S[i % 2][:, :].rearrange("p (n c) -> p n c", n=2),
                    rel[:, :].unsqueeze(1).broadcast_to([P, 2, HEADS * NTOK]), ALU.add).then_inc(s_biased.sem, 1)
                dve.wait_ge(s_biased.sem, s_biased.at(g, i + 1))
                V.tensor_reduce(mx[:, i, :], prob[:, i].rearrange("p n h k -> p (n h) k"), AX.X, ALU.max).then_inc(mx_ready.sem, 1)

            def normalise(g, i):
                dve.wait_ge(pv_done.sem, pv_done.at(g, i + 1))
                ps = B_M[:, 0:4 * PVW].rearrange("p (m c) -> p m c", c=PVW)
                V.reciprocal(r_sum[:, i], ps[:, :, 64:66]).then_inc(rsum_ready.sem, 1)
                dve.wait_ge(rsum_ready.sem, rsum_ready.at(g, i + 1))
                for ab in range(2):
                    rows = slice(C * ab, C * ab + C)
                    V.tensor_tensor(
                        o_n[rows, 2 * i:2 * i + 2, :].rearrange("p n (h j d) -> p (n h) j d", h=2, j=2),
                        ps[rows, :, 32 * ab:32 * ab + 32].rearrange("p m (j d) -> p m j d", j=2),
                        r_sum[rows, i].unsqueeze(3).broadcast_to([C, 4, 2, DH]), ALU.mult).then_inc(on_ready.sem, 1)

            def add_input(g, p):
                dve.wait_ge(proj_done.sem, proj_done.at(g, 1))
                first = (g % (2 * STRIPS)) // STRIPS * C
                planes = xt[:, bass.ds(first, C), bass.ds((g % STRIPS) * ROWS, ROWS)]
                V.tensor_tensor(x2[:, p].rearrange("p (k a) c -> p k a c", a=2),
                                B_M[:, :].rearrange("p (k a c) -> p k a c", a=2, c=C),
                                planes.rearrange("p c (a k) -> p k a c", a=2), ALU.add).then_inc(x2_ready.sem, 1)

            def token_mean(g, p):
                dve.wait_ge(x2_ready.sem, x2_ready.at(g, 1))
                V.tensor_reduce(ln[:, 0, :], x2[:, p], AX.X, ALU.add).then_inc(lsum.sem, 1)
                dve.wait_ge(lsum.sem, lsum.at(g, 1))
                V.tensor_scalar(ln[:, 1, :], ln[:, 0, :], 1.0 / C, None, ALU.mult).then_inc(lsum.sem, 1)

            def token_variance(g):
                dve.wait_ge(xc2_ready.sem, xc2_ready.at(g, 1))
                V.tensor_reduce(ln[:, 2, :], xc2[:, :, :], AX.X, ALU.add).then_inc(lvar.sem, 1)
                dve.wait_ge(lvar.sem, lvar.at(g, 1))
                V.tensor_scalar(ln[:, 2, :], ln[:, 2, :], 1.0 / C, LN_T_EPS, ALU.mult, ALU.add).then_inc(lvar.sem, 1)

            def routing(g):
                dve.wait_ge(logits_done.sem, logits_done.at(g, 1))
                def each(v):
                    return v.unsqueeze(2).broadcast_to([P, ROWS, EXPERTS])

                lg, hot, first, rest, second = (rt[:, n] for n in range(5))
                V.tensor_tensor(lg, B_P[:, 0:ROWS * EXPERTS].rearrange("p (r e) -> p r e", e=EXPERTS), b_rout[:, :, :], ALU.add).then_inc(route.sem, 1)
                dve.wait_ge(route.sem, route.at(g, 1))

                V.tensor_reduce(rs[:, 0, :], lg, AX.X, ALU.max).then_inc(route.sem, 1)
                dve.wait_ge(route.sem, route.at(g, 2))
                V.tensor_tensor(hot, lg, each(rs[:, 0, :]), ALU.is_equal).then_inc(route.sem, 1)
                dve.wait_ge(route.sem, route.at(g, 3))
                V.tensor_tensor(hot, hot, e_rank[:, :, :], ALU.mult).then_inc(route.sem, 1)
                dve.wait_ge(route.sem, route.at(g, 4))
                V.tensor_reduce(rs[:, 7, :], hot, AX.X, ALU.max).then_inc(route.sem, 1)
                dve.wait_ge(route.sem, route.at(g, 5))
                V.tensor_tensor(first, hot, each(rs[:, 7, :]), ALU.is_equal).then_inc(route.sem, 1)
                dve.wait_ge(route.sem, route.at(g, 6))
                V.scalar_tensor_tensor(out=rest, in0=first, scalar=-3.0e38, in1=lg, op0=ALU.mult, op1=ALU.add).then_inc(route.sem, 1)
                dve.wait_ge(route.sem, route.at(g, 7))
                V.tensor_reduce(rs[:, 1, :], rest, AX.X, ALU.max).then_inc(route.sem, 1)
                dve.wait_ge(route.sem, route.at(g, 8))
                V.tensor_tensor(hot, rest, each(rs[:, 1, :]), ALU.is_equal).then_inc(route.sem, 1)
                dve.wait_ge(route.sem, route.at(g, 9))
                V.tensor_tensor(hot, hot, e_rank[:, :, :], ALU.mult).then_inc(route.sem, 1)
                dve.wait_ge(route.sem, route.at(g, 10))
                V.tensor_reduce(rs[:, 7, :], hot, AX.X, ALU.max).then_inc(route.sem, 1)
                dve.wait_ge(route.sem, route.at(g, 11))
                V.tensor_tensor(second, hot, each(rs[:, 7, :]), ALU.is_equal).then_inc(route.sem, 1)
                dve.wait_ge(route.sem, route.at(g, 12))
                V.tensor_tensor(rs[:, 3, :], rs[:, 1, :], rs[:, 0, :], ALU.subtract).then_inc(route.sem, 1)
                dve.wait_ge(route.sem, route.at(g, 13))
                dve.wait_ge(e_ready.sem, e_ready.at(g, 1))
                V.tensor_scalar(rs[:, 5, :], rs[:, 4, :], 1.0, None, ALU.add).then_inc(route.sem, 1)
                dve.wait_ge(route.sem, route.at(g, 14))
                V.reciprocal(rs[:, 5, :], rs[:, 5, :]).then_inc(route.sem, 1)
                dve.wait_ge(route.sem, route.at(g, 15))
                V.tensor_tensor(rs[:, 6, :], rs[:, 4, :], rs[:, 5, :], ALU.mult).then_inc(route.sem, 1)
                dve.wait_ge(route.sem, route.at(g, 16))
                V.tensor_tensor(first, first, each(rs[:, 5, :]), ALU.mult).then_inc(route.sem, 1)
                dve.wait_ge(route.sem, route.at(g, 17))
                V.tensor_tensor(second, second, each(rs[:, 6, :]), ALU.mult).then_inc(route.sem, 1)
                dve.wait_ge(route.sem, route.at(g, 18))
                V.tensor_tensor(lg, first, second, ALU.add).then_inc(route.sem, 1)
                dve.wait_ge(route.sem, route.at(g, 19))
                gates = lg.rearrange("p (k a) e -> p k (a e)", a=2)
                V.tensor_copy(g3[:, :, 0, :], gates).then_inc(route.sem, 1)
                dve.wait_ge(route.sem, route.at(g, 20))
                V.tensor_tensor(gates, gates, g3[:, :, 0, :], ALU.subtract).then_inc(route.sem, 1)
                dve.wait_ge(route.sem, route.at(g, 21))
                V.tensor_copy(g3[:, :, 1, :], gates).then_inc(route.sem, 1)
                dve.wait_ge(route.sem, route.at(g, 22))
                V.tensor_tensor(g3[:, :, 2, :], gates, g3[:, :, 1, :], ALU.subtract).then_inc(route.sem, 1)
                dve.wait_ge(route.sem, route.at(g, 23))

            def gate(g, p, u):
                dve.wait_ge(gate_done.sem, gate_done.at(g, u + 1))
                dve.wait_ge(y_done.sem, y_done.at(g, max(u - TG + 1, 0)))
                V.tensor_tensor(t_g[:, u % TG, :], t_t[:, p, u % 2, :], B_G[:, :], ALU.mult).then_inc(tg_dve.sem, 1)

            def slot(j, p, group, on):
                P_, F_, R_, M_ = ("project" in on, "attend" in on, "route" in on, "mix" in on)
                if R_:
                    token_mean(j - 1, 1 - p)
                if F_:
                    bias_and_max(j, 0)
                    bias_and_max(j, 1)
                if group:
                    take(*group, p)
                if M_:
                    gate(j - 2, p, 0)
                if R_:
                    token_variance(j - 1)
                if M_:
                    gate(j - 2, p, 1)
                if F_:
                    bias_and_max(j, 2)
                if M_:
                    gate(j - 2, p, 2)
                if F_:
                    bias_and_max(j, 3)
                if P_:
                    spread_values(j + 1, 1 - p, 0)
                    spread_values(j + 1, 1 - p, 1)
                if F_:
                    normalise(j, 0)
                if M_:
                    gate(j - 2, p, 4)
                if F_:
                    normalise(j, 1)
                if M_:
                    gate(j - 2, p, 5)
                if F_:
                    normalise(j, 2)
                if M_:
                    gate(j - 2, p, 6)
                if F_:
                    normalise(j, 3)
                if R_:
                    routing(j - 1)
                if F_:
                    add_input(j, p)

            pipeline(dve, slot, take, statistics)

        @block.gpsimd
        def _(pool):
            G = nc.gpsimd
            G.memset(mhalf[:, :], -0.5).then_inc(set_pool.sem, 1)
            pool.wait_ge(set_pool.sem, 1)
            for p in range(2):
                G.memset(q_bd[:, p], 0.0).then_inc(set_pool.sem, 1)
                pool.wait_ge(set_pool.sem, 2 + p)
            G.memset(o_t[C:C + 1, :, :], 1.0).then_inc(set_pool.sem, 1)
            pool.wait_ge(set_pool.sem, SET_POOL)

            def statistics(batch):
                par = batch % 2
                r_std = rstd[:, bass.ds(par, 1), :].rearrange("p o h -> p (o h)")
                pool.wait_ge(stat.sem, stat.at(batch, 6))
                G.tensor_tensor(r_std, st[:, 4, :], mhalf[:, :], ALU.pow).then_inc(rstd_ready.sem, 1)
                pool.wait_ge(rstd_ready.sem, rstd_ready.at(batch, 1))
                G.tensor_tensor(m_rstd[:, bass.ds(par, 1), :].rearrange("p o h -> p (o h)"), st[:, 2, :], r_std,
                                ALU.mult).then_inc(mr_ready.sem, 1)
                pool.wait_ge(mr_ready.sem, mr_ready.at(batch, 1))
                pool.sem_inc(passed, 1)

            def normalise_input(g):
                par = (g % (2 * STRIPS)) // STRIPS
                pool.wait_ge(qkv_done.sem, qkv_done.at(g))
                pool.sem_inc(passed, 1)
                G.tensor_tensor(xn[:, :, :], xt[:, bass.ds((g % (2 * STRIPS)) * 4, 4), :],
                                rstd[:, bass.ds(par, 1), :].broadcast_to([P, 4, H]), ALU.mult).then_inc(xn_ready.sem, 1)
                pool.wait_ge(xn_ready.sem, xn_ready.at(g, 1))
                G.tensor_tensor(xn[:, :, :], xn[:, :, :], m_rstd[:, bass.ds(par, 1), :].broadcast_to([P, 4, H]),
                                ALU.subtract).then_inc(xn_ready.sem, 1)

            def shift(g, i):
                pool.wait_ge(mx_ready.sem, mx_ready.at(g, i + 1))
                sc = prob[:, i].rearrange("p n h k -> p (n h) k")
                G.tensor_tensor(sc, sc, mx[:, i, :].unsqueeze(2).broadcast_to([P, 2 * HEADS, NTOK]),
                                ALU.subtract).then_inc(s_shifted.sem, 1)

            def over_c(v):
                return v.unsqueeze(2).broadcast_to([P, ROWS, C])

            def centre_tokens(g, p):
                pool.wait_ge(lsum.sem, lsum.at(g, 2))
                G.tensor_tensor(xc[:, :, :], x2[:, p], over_c(ln[:, 1, :]), ALU.subtract).then_inc(xc_ready.sem, 1)

            def scale_tokens(g):
                pool.wait_ge(lvar.sem, lvar.at(g, 2))
                G.tensor_tensor(ln[:, 3, :], ln[:, 2, :], mhalf[:, 0:ROWS], ALU.pow).then_inc(lrstd.sem, 1)
                pool.wait_ge(lrstd.sem, lrstd.at(g, 1))
                G.tensor_tensor(t_n[:, :, :], xc[:, :, :], over_c(ln[:, 3, :]), ALU.mult).then_inc(t_ready.sem, 1)

            def gate(g, p, u):
                n = ON_POOL.index(u)
                pool.wait_ge(g_copied.sem, g_copied.at(g, n + 1))
                pool.wait_ge(y_done.sem, y_done.at(g, max(u - TG + 1, 0)))
                G.tensor_tensor(t_g[:, u % TG, :], t_t[:, p, u % 2, :], g_copy[:, n % 2, :],
                                ALU.mult).then_inc(tg_pool.sem, 1)

            def slot(j, p, group, on):
                P_, F_, R_, M_ = ("project" in on, "attend" in on, "route" in on, "mix" in on)
                if R_:
                    centre_tokens(j - 1, 1 - p)
                if F_:
                    shift(j, 0)
                    shift(j, 1)
                if R_:
                    scale_tokens(j - 1)
                if F_:
                    shift(j, 2)
                if M_:
                    gate(j - 2, p, 3)
                if F_:
                    shift(j, 3)
                if P_ and not (isinstance(j, int) and j == STRIPS * BATCH - 2):
                    normalise_input(j + 2)
                if M_:
                    gate(j - 2, p, 7)

            def first_slot(j, p, group, on):
                if isinstance(j, int) and j == -1:
                    normalise_input(0)
                slot(j, p, group, on)

            pipeline(pool, first_slot, lambda batch, t, r: None, statistics)


SET_DVE = 10
SET_POOL = 4
ROUTE_GAP = 13


def rel_index():
    m = np.arange(NTOK)
    r, c = m // 4 % 8, 2 * (m % 4) + m // 32
    return (m[:, None] // WS - r[None, :] + WS - 1) * (2 * WS - 1) + m[:, None] % WS - c[None, :] + WS - 1


_SHAPE = (BATCH, C, H, W)


def kernel(x, L0_conv_Wq, L0_conv_bq, L0_conv_Wkv, L0_conv_bkv, L0_conv_rel_bias, L0_conv_Wproj, L0_conv_bproj,
           L0_ffn_router_w, L0_ffn_router_b, L0_ffn_expert_w, L0_ffn_expert_b):
    import concourse.bacc as _bacc
    from concourse.bass_utils import run_bass_kernel_spmd as _run

    f = np.float32
    a = {k: np.asarray(v) for k, v in dict(
        x=x, wq=L0_conv_Wq, bq=L0_conv_bq, wkv=L0_conv_Wkv, bkv=L0_conv_bkv, rel=L0_conv_rel_bias, wp=L0_conv_Wproj,
        bp=L0_conv_bproj, rw=L0_ffn_router_w, rb=L0_ffn_router_b, ew=L0_ffn_expert_w, eb=L0_ffn_expert_b).items()}
    wqkv = np.concatenate([a["wq"][:, None], a["wkv"].reshape(C, 2, C)], 1)
    qkvb = np.concatenate([a["bq"][:, None], a["bkv"].reshape(2, C).T], 1)
    zero = np.zeros_like(wqkv)
    wexp = a["ew"].reshape(MIXES // 2, 2, C, C).transpose(1, 2, 0, 3).reshape(P, MIXES // 2, C)
    bexp = np.zeros((PARTS, 2, EXPERTS, 2, C), f)
    sel = np.zeros((PARTS, 2, EXPERTS, MIXES, 2, C), f)
    for g in range(2):
        bexp[:, g, :, g, :] = a["eb"]
        for e in range(EXPERTS):
            sel[:, g, e, e // 2 * 2 + g, e % 2, :] = 1.0
    kmask = np.zeros((2, HEADS, DH, HEADS), f)
    kbias = np.zeros((2, HEADS, DH, HEADS), f)
    for h in range(HEADS):
        kmask[:, h, :, h] = 1.0
        kbias[:, h, :, h] = a["bkv"][:C].reshape(HEADS, DH)[h]
    relb = a["rel"][rel_index()].transpose(0, 2, 1).reshape(NTOK, HEADS * NTOK)
    arrays = {
        "x": a["x"],
        "wqkv": np.stack([np.concatenate([wqkv, zero]), np.concatenate([zero, wqkv])], 1),
        "qkvb": np.concatenate([qkvb, qkvb]),
        "kmask": kmask.reshape(P, HEADS),
        "kbias": kbias.reshape(P, HEADS),
        "wproj": np.concatenate([a["wp"], a["bp"][None]]),
        "wrout": a["rw"],
        "brout": np.broadcast_to(a["rb"], (P, ROWS, EXPERTS)),
        "wexp": wexp,
        "bexp": bexp.reshape(GROWS, P),
        "relb": np.concatenate([relb, relb]),
        "ident": np.eye(P, dtype=f),
        "sel": sel.reshape(GROWS, MIXES, P),
        "rank": np.broadcast_to(np.arange(EXPERTS, 0, -1, dtype=f), (P, ROWS, EXPERTS)),
    }
    arrays = {k: np.ascontiguousarray(v) for k, v in arrays.items()}
    nc = _bacc.Bacc("TRN2", target_bir_lowering=False, num_devices=1)
    args = [nc.dram_tensor(f"in_{k}", v.shape, F32, kind="ExternalInput").ap() for k, v in arrays.items()]
    out = nc.dram_tensor("out_y", _SHAPE, F32, kind="ExternalOutput").ap()
    build(nc, *args, out)
    r = _run(nc, [{f"in_{k}": v for k, v in arrays.items()}], core_ids=[0])
    return r.results[0]["out_y"]
```

```python
from contextlib import ExitStack

import numpy as np

import concourse.bass as bass
from concourse import mybir

F32 = mybir.dt.float32
BF16 = mybir.dt.bfloat16
ALU = mybir.AluOpType
ACT = mybir.ActivationFunctionType
AX = mybir.AxisListType

BATCH, C, H, W = 4, 64, 128, 128
P = 128
HEADS, DH = 4, 16
WS = 8
NTOK = WS * WS
STRIPS = C // 4
PAIRS = 8
UNITS = PAIRS // 2
BANK = 512
EXPERTS = 8
MIXES = EXPERTS
ON_POOL = (3, 7)
ON_DVE = tuple(u for u in range(MIXES) if u not in ON_POOL)
TG = 4
ROWS = 8
GROUPS = C // 4
RING = 4
RSTD_PARTS = 4
PVW = 96
PARTS = 3
GROWS = PARTS * 2 * EXPERTS
STAGES = ("project", "attend", "route", "mix")
LN_C_EPS, LN_T_EPS = 1e-6, 1e-5


class Sem:

    def __init__(self, sem, per=1, primed=0):
        self.sem, self.per, self.primed = sem, per, primed

    def at(self, n, k=0):
        return n * self.per + (k + self.primed)


def build(nc, x, wqkv, qkvb, kmask, kbias, wproj, wrout, brout, wexp, bexp, relb, ident, sel, rank, bproj, out):
    ctx = ExitStack()
    with ctx:
        def sb(name, shape, dt=F32):
            return ctx.enter_context(nc.sbuf_tensor(name, shape, dt))

        def sem(name, per=1, primed=0):
            s = Sem(ctx.enter_context(nc.semaphore(name)), per, primed)
            primed_sems.extend([s] * primed)
            return s

        primed_sems = []

        w_qkv = sb("w_qkv", [P, 2, 3, C])
        b_qkv = sb("b_qkv", [P, 3])
        q_bias = sb("q_bias", [P, 1])
        k_mask = sb("k_mask", [P, HEADS])
        k_bias = sb("k_bias", [P, HEADS])
        w_proj = sb("w_proj", [P, 2, C])
        b_proj = sb("b_proj", [C + 1, BANK])
        b_proj_part = sb("b_proj_part", [C + 1, BANK], BF16)
        part_now = sb("part_now", [C + 1, BANK], BF16)
        ones16 = sb("ones16", [C + 1, P], BF16)
        w_rout = sb("w_rout", [P, 2 * EXPERTS])
        b_rout = sb("b_rout", [P, ROWS, EXPERTS])
        w_exp = sb("w_exp", [P, MIXES // 2, C])
        b_exp = sb("b_exp", [GROWS, P])
        b_exp_part = sb("b_exp_part", [GROWS, PARTS, P], BF16)
        rel = sb("rel", [P, HEADS * NTOK])
        idn = sb("idn", [P, P])
        idn16 = sb("idn16", [P, P], BF16)
        gate_sel = sb("gate_sel", [GROWS, MIXES, P])
        gate_sel16 = sb("gate_sel16", [GROWS, MIXES, P], BF16)
        e_rank = sb("e_rank", [P, ROWS, EXPERTS])
        mhalf = sb("mhalf", [P, H])

        x_in = sb("x_in", [P, RING, 4, W])
        xt = sb("xt", [P, 2 * C, H])
        x_sq = sb("x_sq", [P, 2, 4, H])
        sums = sb("sums", [P, H, GROUPS // 2])
        sums2 = sb("sums2", [P, H, GROUPS // 2])
        st = sb("st", [P, 5, H])
        rstd = sb("rstd", [P, 2, H])
        m_rstd = sb("m_rstd", [P, 2, H])

        xn = sb("xn", [P, 4, H])
        q_bd = sb("q_bd", [P, 2, PAIRS, 2 * NTOK])
        k_m = sb("k_m", [P, 2, PAIRS, HEADS, NTOK])
        v_t = sb("v_t", [P, PAIRS + 1, NTOK])
        v_bd = sb("v_bd", [P, 2, PAIRS, 2, PVW])
        prob = sb("prob", [P, UNITS, 2, HEADS, NTOK])
        mx = sb("mx", [P, UNITS, 2 * HEADS])
        prob_t = sb("prob_t", [P, 2, 2, 2, P])
        r_sum = sb("r_sum", [P, UNITS, 4, 2])
        o_n = sb("o_n", [P, PAIRS, C])
        o_t = sb("o_t", [P, 4, W])
        x2 = sb("x2", [P, 2, ROWS, C])

        ln = sb("ln", [P, 4, ROWS])
        xc = sb("xc", [P, ROWS, C])
        xc2 = sb("xc2", [P, ROWS, C])
        t_n = sb("t_n", [P, ROWS, C])
        t_rout = sb("t_rout", [P, BANK])
        t_t = sb("t_t", [P, 2, 2, BANK])
        rt = sb("rt", [P, 5, ROWS, EXPERTS])
        rs = sb("rs", [P, 6, ROWS])
        g3 = sb("g3", [P, 4, PARTS, 2 * EXPERTS], BF16)
        g_t = sb("g_t", [GROWS, BANK], BF16)
        t_g = sb("t_g", [P, TG, BANK])
        g_copy = sb("g_copy", [P, 2, BANK])
        y_out = sb("y_out", [P, 4, W])

        bank = [ctx.enter_context(nc.psum_tensor(f"bank{i}", [P, BANK], F32)) for i in range(8)]
        B_S = bank[0:2]
        B_T = bank[2:4]
        B_M = bank[4]
        B_P = bank[5]
        B_G = bank[6]
        B_Y = bank[7]

        idn_loaded = ctx.enter_context(nc.semaphore("idn_loaded"))
        loads = ctx.enter_context(nc.semaphore("weights_loaded"))
        x_loaded = [Sem(ctx.enter_context(nc.semaphore(f"x_loaded{r}"))) for r in range(RING)]
        passed = ctx.enter_context(nc.semaphore("passed"))
        stored = ctx.enter_context(nc.semaphore("stored"))
        set_pool = sem("set_pool")
        set_dve = sem("set_dve")
        set_act = sem("set_act")
        x_turned = sem("x_turned")
        xt_ready = sem("xt_ready", primed=1)
        sq_ready = sem("sq_ready")
        part_sums = sem("part_sums", primed=1)
        stat = sem("stat", 6)
        rstd_ready = sem("rstd_ready", RSTD_PARTS)
        root_ready = sem("root_ready")
        newton = sem("newton", 4)
        mr_ready = sem("mr_ready")

        xn_ready = sem("xn_ready", 2)
        qkv_done = sem("qkv_done", 3, primed=1)
        q_ready = sem("q_ready", 4)
        k_ready = sem("k_ready", 4)
        v_ready = sem("v_ready", 2)
        vrow_done = sem("vrow_done", 2)
        vbd_ready = sem("vbd_ready", 10, primed=1)
        s_done = sem("s_done", UNITS)
        s_biased = sem("s_biased", UNITS, primed=1)
        mx_ready = sem("mx_ready", UNITS)
        s_shifted = sem("s_shifted", UNITS)
        p_ready = sem("p_ready", UNITS)
        pt_done = sem("pt_done", UNITS)
        pt_ready = sem("pt_ready", UNITS)
        pv_done = sem("pv_done", UNITS, primed=1)
        rsum_ready = sem("rsum_ready", UNITS)
        on_ready = sem("on_ready", 2 * UNITS)
        ot_done = sem("ot_done", 2)
        ot_ready = sem("ot_ready", 8, primed=1)
        proj_done = sem("proj_done")
        x2_ready = sem("x2_ready", primed=1)

        lsum = sem("lsum", 2)
        xc_ready = sem("xc_ready")
        xc2_ready = sem("xc2_ready")
        lvar = sem("lvar", 2)
        lrstd = sem("lrstd")
        t_ready = sem("t_ready")
        tt_done = sem("tt_done")
        tt_ready = sem("tt_ready", 5)
        logits_done = sem("logits_done")
        route = sem("route", 22)
        e_ready = sem("e_ready")
        gt_done = sem("gt_done")
        gt_ready = sem("gt_ready")
        gate_done = sem("gate_done", MIXES)
        g_copied = sem("g_copied", len(ON_POOL))
        tg_dve = sem("tg_dve", MIXES - len(ON_POOL), primed=1)
        tg_pool = sem("tg_pool", len(ON_POOL))
        y_done = sem("y_done", MIXES, primed=1)
        y_ready = sem("y_ready", primed=1)

        consts = [(w_qkv, wqkv), (b_qkv, qkvb), (k_mask, kmask), (k_bias, kbias), (w_proj, wproj), (w_rout, wrout),
                  (b_rout, brout), (w_exp, wexp), (b_exp, bexp), (rel, relb),
                  (gate_sel, sel), (e_rank, rank), (b_proj, bproj)]
        ALL_LOADED = 16 * len(consts)

        block = ctx.enter_context(nc.Block())

        def turned(ap):
            return ap.rearrange("p (a v l) -> p v a l", v=PAIRS, l=4)

        def pipeline(eng, slot, take, sum_up, statistics):
            all_on = STAGES
            with eng.Fori(0, 4) as t:
                for r in range(2):
                    take(0, t, r)
            sum_up(0)
            statistics(0)
            slot(-1, 1, None, all_on[:1])
            slot(0, 0, None, all_on[:2])
            slot(1, 1, None, all_on[:3])
            with eng.Fori(0, BATCH - 1) as b:
                with eng.Fori(0, 4) as t:
                    for r in range(2):
                        slot(b * STRIPS + t * 2 + (2 + r), r, ("take", b + 1, t, r), all_on)
                sum_up(b + 1)
                with eng.Fori(4, 6) as t:
                    for r in range(2):
                        slot(b * STRIPS + t * 2 + (2 + r), r, ("power", b + 1, t * 2 + (r - 8)), all_on)
                statistics(b + 1)
                with eng.Fori(6, 8) as t:
                    for r in range(2):
                        slot(b * STRIPS + t * 2 + (2 + r), r, None, all_on)
            with eng.Fori(0, 6) as t:
                for r in range(2):
                    slot(t * 2 + (STRIPS * (BATCH - 1) + 2 + r), r, None, all_on)
            slot(LAST - 1, 0, None, all_on)
            slot(LAST, 1, None, all_on[1:])
            slot(LAST + 1, 0, None, all_on[2:])
            slot(LAST + 2, 1, None, all_on[3:])

        @block.sync
        def _(sp):
            for s in primed_sems:
                sp.sem_inc(s.sem, 1)
            sp.sem_inc(stored, 1)
            xg = x.rearrange("b (q c) h w -> (b q) h c w", c=4)
            sp.dma_start(idn[:, :], ident).then_inc(idn_loaded, 16)
            for r in range(RING):
                sp.dma_start(x_in[:, r], xg[r]).then_inc(x_loaded[r].sem, 16)
            for dst, src in consts:
                sp.dma_start(dst[tuple(slice(None) for _ in dst.shape)], src).then_inc(loads, 16)

            def load(n, first, count):
                for r in range(first, first + count):
                    sp.wait_ge(x_turned.sem, x_turned.at(n - RING, r + 1))
                    sp.dma_start(x_in[:, r], xg[bass.ds(n + r, 1)].rearrange("o h c w -> h (o c) w")
                                 ).then_inc(x_loaded[r].sem, 16)

            def store(b, s):
                sp.wait_ge(y_ready.sem, y_ready.at(b * STRIPS + s, 1))
                for a in range(2):
                    dst = out[bass.ds(b, 1), :, bass.ds(s * ROWS + 4 * a, 4), :]
                    sp.dma_start(dst.rearrange("o c k w -> (o c) k w"), y_out[C * a:C * a + C]).then_inc(stored, 16)

            with sp.Fori(1, GROUPS // RING) as t:
                load(t * RING, 0, RING)
            with sp.Fori(0, BATCH - 1) as b:
                load(b * GROUPS + GROUPS, 0, RING)
                with sp.Fori(1, GROUPS // RING) as t:
                    for r in range(2):
                        load(b * GROUPS + GROUPS + t * RING, 2 * r, 2)
                        store(b, t * 2 + (r - 2))
                with sp.Fori(GROUPS // RING - 1, STRIPS // 2) as t:
                    for r in range(2):
                        store(b, t * 2 + r)
            with sp.Fori(0, STRIPS) as t:
                store(BATCH - 1, t)
            sp.wait_ge(stored, BATCH * STRIPS * 32 + 1)

        @block.tensor
        def _(pe):
            mm, tr = nc.tensor.matmul, nc.tensor.transpose
            pe.wait_ge(idn_loaded, 16)

            def take(batch, t, r, g=None):
                for m in range(2):
                    n = 2 * r + m
                    pe.wait_ge(x_loaded[n].sem, (batch * (GROUPS // RING) + t + 1) * 16)
                    if g is None:
                        pe.wait_ge(xt_ready.sem, xt_ready.at(t * RING, max(n - 1, 0)))
                    else:
                        pe.wait_ge(ot_ready.sem, ot_ready.at(g, 4 * m + 4))
                    for c in range(4):
                        last = tr(B_T[m][:, c * H:(c + 1) * H], x_in[:, n, c, :], idn[:, :])
                    last.then_inc(x_turned.sem, 1)

            def project(g, i, dst):
                if i == 1:
                    pe.wait_ge(xn_ready.sem, xn_ready.at(g, 2))
                    if isinstance(g, int) and g == 1:
                        pe.wait_ge(k_ready.sem, k_ready.at(1))
                    elif not (isinstance(g, int) and g == 0):
                        pe.wait_ge(x2_ready.sem, x2_ready.at(g - 1))
                elif i == 0 and not (isinstance(g, int) and g < 3):
                    pe.wait_ge(gt_ready.sem, gt_ready.at(g - 3, 1))
                elif i == 0 and not (isinstance(g, int) and g == 0):
                    pe.wait_ge(v_ready.sem, v_ready.at(g))
                elif i == 2:
                    pe.wait_ge(q_ready.sem, q_ready.at(g, 4))
                for half in range(2):
                    for ab in range(2):
                        src = xn[:, :, :].rearrange("p c (hh ab l) -> p (c hh) ab l", ab=2, l=32)[:, :, ab, :]
                        last = mm(dst[C * ab:C * ab + C, 256 * half:256 * half + 256], w_qkv[:, half, i, :], src,
                                  start=True, stop=True, skip_group_check=True)
                last.then_inc(qkv_done.sem, 1)

            def turn_values(g, u):
                dst = B_S[u]
                pe.wait_ge(v_ready.sem, v_ready.at(g, 2))
                if not (isinstance(g, int) and g == 0):
                    pe.wait_ge(s_biased.sem, s_biased.at(g - 1, 3 + u))
                for n in range(4):
                    v = 4 * u + n
                    last = tr(dst[:, n * P:(n + 1) * P], v_t[:, v:v + 2, :].rearrange("p v t -> p (v t)"), idn[:, :])
                last.then_inc(vrow_done.sem, 1)

            def scores(g, p, i):
                if i == 0:
                    pe.wait_ge(q_ready.sem, q_ready.at(g, 4))
                    pe.wait_ge(k_ready.sem, k_ready.at(g, 4))
                if i < 2:
                    pe.wait_ge(vbd_ready.sem, vbd_ready.at(g, (4, 10)[i]))
                else:
                    pe.wait_ge(s_biased.sem, s_biased.at(g, i - 1))
                for n in range(2):
                    v = 2 * i + n
                    last = mm(B_S[i % 2][:, n * 256:(n + 1) * 256], q_bd[:, p, v, :],
                              k_m[:, p, v, :, :].rearrange("p h k -> p (h k)"), start=True, stop=True,
                              skip_group_check=True)
                last.then_inc(s_done.sem, 1)

            def turn_probs(g, i, group):
                pe.wait_ge(p_ready.sem, p_ready.at(g, i + 1))
                if i >= 2:
                    pe.wait_ge(pt_ready.sem, pt_ready.at(g, i - 1))
                elif group and group[0] == "take":
                    pe.wait_ge(xt_ready.sem, xt_ready.at(group[1] * GROUPS + group[2] * RING, 2 * group[3] + i + 1))
                elif not (isinstance(g, int) and g == 0):
                    pe.wait_ge(ot_ready.sem, ot_ready.at(g - 1, 4 * i + 4))
                for n in range(2):
                    for hp in range(2):
                        at = (2 * n + hp) * P
                        last = tr(B_T[i % 2][:, at:at + P],
                                  prob[:, i, n, 2 * hp:2 * hp + 2, :].rearrange("p h k -> p (h k)"), idn[:, :])
                last.then_inc(pt_done.sem, 1)

            def values(g, p, i):
                pe.wait_ge(pt_ready.sem, pt_ready.at(g, i + 1))
                if i:
                    pe.wait_ge(on_ready.sem, on_ready.at(g, 2 * i))
                elif not (isinstance(g, int) and g == LAST):
                    pe.wait_ge(k_ready.sem, k_ready.at(g + 1, 4))
                else:
                    pe.wait_ge(x2_ready.sem, x2_ready.at(g))
                for n in range(2):
                    for hp in range(2):
                        at = (2 * n + hp) * PVW
                        last = mm(B_M[:, at:at + PVW], prob_t[:, i % 2, n, hp, :], v_bd[:, p, 2 * i + n, hp, :],
                                  start=True, stop=True, skip_group_check=True)
                last.then_inc(pv_done.sem, 1)

            def turn_outputs(g, u):
                pe.wait_ge(on_ready.sem, on_ready.at(g, 4 * u + 4))
                pe.wait_ge(pt_ready.sem, pt_ready.at(g, 3 + u))
                pe.sem_inc(passed, 1)
                for n in range(4):
                    last = tr(B_T[u][0:C, n * P:(n + 1) * P], o_n[:, 4 * u + n, :], idn[:, :])
                last.then_inc(ot_done.sem, 1)

            def project_out(g):
                pe.wait_ge(ot_ready.sem, ot_ready.at(g, 8))
                pe.wait_ge(on_ready.sem, on_ready.at(g, 8))
                mm(B_M[:, :], ones16[:, :], b_proj_part[:, :], start=True, stop=False, skip_group_check=True)
                for k in range(4):
                    last = mm(B_M[:, k * P:(k + 1) * P], o_t[:, k, :], w_proj[:, :, :].rearrange("p a c -> p (a c)"),
                              start=False, stop=(k == 3), skip_group_check=True)
                last.then_inc(proj_done.sem, 1)

            def turn_tokens(g):
                pe.wait_ge(t_ready.sem, t_ready.at(g, 1))
                if not (isinstance(g, int) and g > LAST - 2):
                    pe.wait_ge(v_ready.sem, v_ready.at(g + 2, 2))
                else:
                    pe.wait_ge(gt_ready.sem, gt_ready.at(g - 1, 1))
                for k in range(4):
                    src = t_n[:, 2 * k:2 * k + 2, :].rearrange("p a c -> p (a c)")
                    last = tr(B_P[:, k * P:(k + 1) * P], src, idn[:, :])
                last.then_inc(tt_done.sem, 1)

            def logits(g):
                pe.wait_ge(tt_ready.sem, tt_ready.at(g, 5))
                for k in range(4):
                    at = 2 * k * EXPERTS
                    last = mm(B_P[:, at:at + 2 * EXPERTS], t_rout[:, k * P:(k + 1) * P], w_rout[:, :],
                              start=True, stop=True, skip_group_check=True)
                last.then_inc(logits_done.sem, 1)

            def turn_gates(g):
                pe.wait_ge(route.sem, route.at(g, route.per))
                pe.sem_inc(passed, 1)
                gt16 = B_P[:, :].bitcast(BF16)
                for k in range(4):
                    last = tr(gt16[0:GROWS, k * P:(k + 1) * P], g3[:, k].rearrange("p a e -> p (a e)"), idn16[:, :])
                last.then_inc(gt_done.sem, 1)

            def start_sum(g, p):
                pe.wait_ge(y_ready.sem, y_ready.at(g))
                for k in range(4):
                    src = x2[:, p, 2 * k:2 * k + 2, :].rearrange("p a c -> p (a c)")
                    mm(B_Y[:, k * P:(k + 1) * P], src, idn[:, :], is_transpose=True, start=(k == 0), stop=False,
                       skip_group_check=True)
                pe.wait_ge(gt_ready.sem, gt_ready.at(g, 1))
                for part in range(PARTS):
                    mm(B_Y[:, :], b_exp_part[:, part, :], g_t[:, :], start=False, stop=False, skip_group_check=True)

            def gates(g, u):
                if u and u - 1 in ON_POOL:
                    pe.wait_ge(g_copied.sem, g_copied.at(g, ON_POOL.index(u - 1) + 1))
                elif u:
                    pe.wait_ge(tg_dve.sem, tg_dve.at(g, ON_DVE.index(u - 1) + 1))
                mm(B_G[:, :], gate_sel16[:, u, :], g_t[:, :], start=True, stop=True).then_inc(gate_done.sem, 1)

            def experts(g, pair):
                for a in range(2):
                    u = 2 * pair + a
                    if u in ON_POOL:
                        pe.wait_ge(tg_pool.sem, tg_pool.at(g, ON_POOL.index(u) + 1))
                    else:
                        pe.wait_ge(tg_dve.sem, tg_dve.at(g, ON_DVE.index(u) + 1))
                for a in range(2):
                    mm(B_Y[C * a:C * a + C, :], w_exp[:, pair, :], t_g[:, (2 * pair + a) % TG, :], start=False,
                       stop=(pair == MIXES // 2 - 1), skip_group_check=True).then_inc(y_done.sem, 1)

            def slot(j, p, group, on):
                projecting, attending, routing_on, mixing = (stage in on for stage in STAGES)
                if isinstance(j, int) and j == 0:
                    pe.wait_ge(set_dve.sem, SET_DVE)
                if mixing:
                    turn_gates(j - 2)
                if projecting:
                    project(j + 1, 1, B_M)
                if attending:
                    scores(j, p, 1)
                if projecting:
                    project(j + 1, 0, B_P)
                if group and group[0] == "take":
                    take(group[1], group[2], p, j - 1)
                if attending:
                    scores(j, p, 2)
                if mixing:
                    start_sum(j - 2, p)
                    gates(j - 2, 0)
                if attending:
                    scores(j, p, 3)
                    turn_probs(j, 0, group)
                if mixing:
                    gates(j - 2, 1)
                if projecting:
                    project(j + 1, 2, B_P)
                if mixing:
                    gates(j - 2, 2)
                if attending:
                    values(j, p, 0)
                    turn_probs(j, 1, group)
                if projecting:
                    turn_values(j + 1, 0)
                if mixing:
                    gates(j - 2, 3)
                if routing_on:
                    turn_tokens(j - 1)
                if projecting:
                    turn_values(j + 1, 1)
                if attending:
                    values(j, p, 1)
                    turn_probs(j, 2, group)
                if mixing:
                    experts(j - 2, 0)
                    gates(j - 2, 4)
                if routing_on:
                    logits(j - 1)
                if attending:
                    turn_probs(j, 3, group)
                if mixing:
                    gates(j - 2, 5)
                if attending:
                    values(j, p, 2)
                if mixing:
                    experts(j - 2, 1)
                    gates(j - 2, 6)
                if attending:
                    turn_outputs(j, 0)
                    values(j, p, 3)
                if mixing:
                    gates(j - 2, 7)
                if projecting:
                    scores(j + 1, 1 - p, 0)
                if attending:
                    turn_outputs(j, 1)
                if mixing:
                    experts(j - 2, 2)
                if attending:
                    project_out(j)
                if mixing:
                    experts(j - 2, 3)

            def weights(batch):
                if isinstance(batch, int):
                    pe.wait_ge(loads, ALL_LOADED)
                    pe.wait_ge(set_pool.sem, SET_POOL)

            pipeline(pe, slot, take, weights, lambda batch: None)

        @block.scalar
        def _(act):
            A = nc.scalar.activation

            def take(batch, t, r):
                n = batch * GROUPS + t * RING
                plane = (n % (2 * GROUPS)) * 4
                for m in range(2):
                    dst = xt[:, bass.ds(plane + (2 * r + m) * 4, 4), :]
                    act.wait_ge(x_turned.sem, x_turned.at(n, 2 * r + m + 1))
                    act.sem_inc(passed, 1)
                    A(dst, B_T[m][:, :].rearrange("p (c h) -> p c h", c=4), ACT.Copy).then_inc(xt_ready.sem, 1)
                for m in range(2):
                    act.wait_ge(xt_ready.sem, xt_ready.at(n, 2 * r + m + 1))
                    act.wait_ge(part_sums.sem, part_sums.at(n + 2 * r))
                    act.sem_inc(passed, 1)
                    A(x_sq[:, m], xt[:, bass.ds(plane + (2 * r + m) * 4, 4), :], ACT.Square).then_inc(sq_ready.sem, 1)

            def first_root(batch):
                if isinstance(batch, int):
                    act.wait_ge(loads, ALL_LOADED)
                    A(q_bias[:, :], b_qkv[:, 0:1], ACT.Copy, scale=float(DH) ** -0.5).then_inc(set_act.sem, 1)
                    act.wait_ge(set_act.sem, 1)
                    act.wait_ge(set_pool.sem, SET_POOL)
                    act.wait_ge(stat.sem, stat.at(0, 6))
                    A(rstd[:, 1, :], st[:, 4, :], ACT.Sqrt).then_inc(root_ready.sem, 1)

            def copy_q(g, p):
                act.wait_ge(qkv_done.sem, qkv_done.at(g, 2))
                for ab in range(2):
                    rows = slice(C * ab, C * ab + C)
                    for half in range(2):
                        A(q_bd[rows, p, :, ab * NTOK:(ab + 1) * NTOK].rearrange("p v (r l a) -> p v r l a", a=2, l=4)[
                            :, :, :, :, half],
                          turned(B_P[rows, 256 * half:256 * half + 256]), ACT.Identity, bias=q_bias[rows, :],
                          scale=float(DH) ** -0.5).then_inc(q_ready.sem, 1)

            def copy_k(g, p):
                act.wait_ge(qkv_done.sem, qkv_done.at(g, 1))
                for h in range(HEADS):
                    A(k_m[:, p, :, h, :].rearrange("p v (a l) -> p v a l", l=4), turned(B_M[:, :]), ACT.Identity,
                      bias=k_bias[:, h:h + 1], scale=k_mask[:, h:h + 1]).then_inc(k_ready.sem, 1)

            def copy_v(g):
                act.wait_ge(qkv_done.sem, qkv_done.at(g, 3))
                A(v_t[:, 0:PAIRS, :].rearrange("p v (a l) -> p v a l", l=4), turned(B_P[:, :]), ACT.Identity,
                  bias=b_qkv[:, 2:3]).then_inc(v_ready.sem, 1)
                A(v_t[:, PAIRS, :].rearrange("p (a l) -> p a l", l=4), turned(B_P[:, :])[:, 0], ACT.Identity,
                  bias=b_qkv[:, 2:3]).then_inc(v_ready.sem, 1)

            def exps(g, i):
                act.wait_ge(s_shifted.sem, s_shifted.at(g, i + 1))
                A(prob[:, i], prob[:, i], ACT.Exp).then_inc(p_ready.sem, 1)

            def copy_probs(g, i):
                act.wait_ge(pt_done.sem, pt_done.at(g, i + 1))
                act.wait_ge(pv_done.sem, pv_done.at(g, max(i - 1, 0)))
                A(prob_t[:, i % 2].rearrange("p n h q -> p (n h q)"), B_T[i % 2][:, :],
                  ACT.Copy).then_inc(pt_ready.sem, 1)

            def copy_outputs(g, u):
                act.wait_ge(ot_done.sem, ot_done.at(g, u + 1))
                for ab in range(2):
                    at = (PAIRS * ab + 4 * u) * WS
                    for a in range(2):
                        A(o_t[C * a:C * a + C, :, at:at + 4 * WS].rearrange("c k (v s) -> c v k s", s=WS),
                          B_T[u][0:C, :].rearrange("c (v ab a k s) -> c ab a v k s", v=4, ab=2, a=2, s=WS)[:, ab, a],
                          ACT.Copy).then_inc(ot_ready.sem, 1)

            def square(g):
                act.wait_ge(xc_ready.sem, xc_ready.at(g, 1))
                A(xc2[:, :, :], xc[:, :, :], ACT.Square).then_inc(xc2_ready.sem, 1)

            def copy_tokens(g, p):
                act.wait_ge(tt_done.sem, tt_done.at(g, 1))
                A(t_rout[:, :], B_P[:, :], ACT.Copy).then_inc(tt_ready.sem, 1)
                for a in range(2):
                    for copy in range(2):
                        A(t_t[C * copy:C * copy + C, p, a, :], B_P[C * a:C * a + C, :],
                          ACT.Copy).then_inc(tt_ready.sem, 1)

            def gate_exp(g):
                act.wait_ge(route.sem, route.at(g, ROUTE_GAP))
                A(rs[:, 3, :], rs[:, 2, :], ACT.Exp).then_inc(e_ready.sem, 1)

            def copy_turned_gates(g):
                act.wait_ge(gt_done.sem, gt_done.at(g, 1))
                A(g_t[:, :], B_P[:, :].bitcast(BF16)[0:GROWS, 0:BANK], ACT.Copy).then_inc(gt_ready.sem, 1)

            def copy_gates(g, u):
                act.wait_ge(gate_done.sem, gate_done.at(g, u + 1))
                A(g_copy[:, ON_POOL.index(u) % 2, :], B_G[:, :], ACT.Copy).then_inc(g_copied.sem, 1)

            def copy_result(g):
                act.wait_ge(y_done.sem, y_done.at(g, MIXES))
                act.wait_ge(stored, g * 32 + 1)
                A(y_out[:, :, :].rearrange("p k w -> p (k w)"), B_Y[:, :], ACT.Copy).then_inc(y_ready.sem, 1)

            def slot(j, p, group, on):
                projecting, attending, routing_on, mixing = (stage in on for stage in STAGES)
                if mixing:
                    copy_turned_gates(j - 2)
                if projecting:
                    copy_k(j + 1, 1 - p)
                if attending:
                    exps(j, 0)
                if routing_on:
                    square(j - 1)
                if projecting:
                    copy_q(j + 1, 1 - p)
                if group and group[0] == "take":
                    take(group[1], group[2], p)
                if attending:
                    copy_probs(j, 0)
                    exps(j, 1)
                if projecting:
                    copy_v(j + 1)
                if attending:
                    exps(j, 2)
                    copy_probs(j, 1)
                if mixing:
                    copy_gates(j - 2, 3)
                if routing_on:
                    copy_tokens(j - 1, 1 - p)
                if attending:
                    exps(j, 3)
                    copy_probs(j, 2)
                    copy_probs(j, 3)
                if routing_on:
                    gate_exp(j - 1)
                if attending:
                    copy_outputs(j, 0)
                if mixing:
                    copy_gates(j - 2, 7)
                if attending:
                    copy_outputs(j, 1)
                if mixing:
                    copy_result(j - 2)

            pipeline(act, slot, take, first_root, lambda batch: None)

        @block.vector
        def _(dve):
            V = nc.vector
            V.memset(v_bd[:, :, :, :, :], 0.0).then_inc(set_dve.sem, 1)
            dve.wait_ge(set_dve.sem, 1)
            for j in range(2):
                V.memset(v_bd[C * j:C * j + C, :, :, :, 64 + j:65 + j], 1.0).then_inc(set_dve.sem, 1)

            def prepare_weights():
                dve.wait_ge(loads, ALL_LOADED)
                dve.wait_ge(idn_loaded, 16)
                V.tensor_copy(idn16[:, :], idn[:, :]).then_inc(set_dve.sem, 1)
                V.tensor_copy(gate_sel16[:, :, :], gate_sel[:, :, :]).then_inc(set_dve.sem, 1)
                V.tensor_copy(b_exp_part[:, 0, :], b_exp[:, :]).then_inc(set_dve.sem, 1)
                for part in range(1, PARTS):
                    dve.wait_ge(set_dve.sem, 4 + 2 * part)
                    V.tensor_tensor(b_exp[:, :], b_exp[:, :], b_exp_part[:, part - 1, :],
                                    ALU.subtract).then_inc(set_dve.sem, 1)
                    dve.wait_ge(set_dve.sem, 5 + 2 * part)
                    V.tensor_copy(b_exp_part[:, part, :], b_exp[:, :]).then_inc(set_dve.sem, 1)

                done = 10
                V.memset(ones16[:, :], 1.0).then_inc(set_dve.sem, 1)
                V.memset(b_proj_part[:, :], 0.0).then_inc(set_dve.sem, 1)
                for part, row in enumerate(PART_ROWS):
                    V.tensor_copy(part_now[:, :], b_proj[:, :]).then_inc(set_dve.sem, 1)
                    dve.wait_ge(set_dve.sem, done + 3 + 3 * part)
                    V.tensor_copy(b_proj_part[row:row + 1, :], part_now[row:row + 1, :]).then_inc(set_dve.sem, 1)
                    if part < PARTS - 1:
                        V.tensor_tensor(b_proj[:, :], b_proj[:, :], part_now[:, :], ALU.subtract).then_inc(set_dve.sem, 1)
                        dve.wait_ge(set_dve.sem, done + 5 + 3 * part)
                dve.wait_ge(set_dve.sem, SET_DVE)

            def take(batch, t, r):
                n = batch * GROUPS + t * RING
                plane = (n % (2 * GROUPS)) * 4
                pair = bass.ds(t * 2 + r, 1)
                dve.wait_ge(xt_ready.sem, xt_ready.at(n, 2 * r + 2))
                V.tensor_reduce(sums[:, :, pair].rearrange("p h o -> p (h o)"),
                                xt[:, bass.ds(plane + 8 * r, 8), :].rearrange("p c h -> p h c"),
                                AX.X, ALU.add).then_inc(part_sums.sem, 1)
                dve.wait_ge(sq_ready.sem, sq_ready.at(n, 2 * r + 2))
                V.tensor_reduce(sums2[:, :, pair].rearrange("p h o -> p (h o)"),
                                x_sq[:, :, :, :].rearrange("p m c h -> p h (m c)"), AX.X,
                                ALU.add).then_inc(part_sums.sem, 1)

            def statistics(batch):
                par = batch % 2
                dve.wait_ge(part_sums.sem, part_sums.at(batch * GROUPS + GROUPS))
                V.tensor_reduce(st[:, 0, :], sums[:, :, :], AX.X, ALU.add).then_inc(stat.sem, 1)
                V.tensor_reduce(st[:, 1, :], sums2[:, :, :], AX.X, ALU.add).then_inc(stat.sem, 1)
                dve.wait_ge(stat.sem, stat.at(batch, 2))
                V.tensor_scalar(st[:, 2, :], st[:, 0, :], 1.0 / C, None, ALU.mult).then_inc(stat.sem, 1)
                dve.wait_ge(stat.sem, stat.at(batch, 3))
                V.tensor_tensor(st[:, 3, :], st[:, 2, :], st[:, 2, :], ALU.mult).then_inc(stat.sem, 1)
                dve.wait_ge(stat.sem, stat.at(batch, 4))
                V.scalar_tensor_tensor(out=st[:, 4, :], in0=st[:, 1, :], scalar=1.0 / C, in1=st[:, 3, :],
                                       op0=ALU.mult, op1=ALU.subtract).then_inc(stat.sem, 1)
                dve.wait_ge(stat.sem, stat.at(batch, 5))
                V.tensor_scalar(st[:, 4, :], st[:, 4, :], 0.0, LN_C_EPS, ALU.max, ALU.add).then_inc(stat.sem, 1)

            def first_deviations():
                r_std, v, half = rstd[:, 0, :], st[:, 4, :], x_sq[:, 0, 0, :]
                dve.wait_ge(root_ready.sem, 1)
                V.reciprocal(r_std, rstd[:, 1, :]).then_inc(newton.sem, 1)
                dve.wait_ge(newton.sem, 1)
                V.tensor_tensor(half, v, r_std, ALU.mult).then_inc(newton.sem, 1)
                dve.wait_ge(newton.sem, 2)
                V.tensor_tensor(half, half, r_std, ALU.mult).then_inc(newton.sem, 1)
                dve.wait_ge(newton.sem, 3)
                V.tensor_scalar(half, half, -0.5, 1.5, ALU.mult, ALU.add).then_inc(newton.sem, 1)
                dve.wait_ge(newton.sem, 4)
                V.tensor_tensor(r_std, r_std, half, ALU.mult).then_inc(rstd_ready.sem, RSTD_PARTS)

            def sum_up(batch):
                statistics(batch)
                if isinstance(batch, int):
                    first_deviations()
                    prepare_weights()

            def spread_values(g, p, u):
                dve.wait_ge(vrow_done.sem, vrow_done.at(g, u + 1))
                src = B_S[u]
                runs = [(0, 0, 4, 4 * u), (1, 0, 4, 1)] if u == 0 else [(0, 0, 4, 4), (1, 0, 3, 5), (1, 3, 1, 0)]
                for j, n0, count, v0 in runs:
                    rows = slice(C * j, C * j + C)
                    for hp in range(2):
                        at = (2 * hp + j) * DH
                        V.tensor_copy(
                            v_bd[rows, p, v0:v0 + count, hp, 0:64].rearrange("p v (ab c) -> p v ab c", ab=2)[
                                :, :, :, j * DH:(j + 1) * DH],
                            src[rows, :].rearrange("p (v ab c) -> p v ab c", v=4, ab=2)[
                                :, n0:n0 + count, :, at:at + DH]).then_inc(vbd_ready.sem, 1)

            def bias_and_max(g, i):
                dve.wait_ge(s_done.sem, s_done.at(g, i + 1))
                V.tensor_tensor(
                    prob[:, i].rearrange("p n h k -> p n (h k)"), B_S[i % 2][:, :].rearrange("p (n c) -> p n c", n=2),
                    rel[:, :].unsqueeze(1).broadcast_to([P, 2, HEADS * NTOK]), ALU.add).then_inc(s_biased.sem, 1)
                dve.wait_ge(s_biased.sem, s_biased.at(g, i + 1))
                V.tensor_reduce(mx[:, i, :], prob[:, i].rearrange("p n h k -> p (n h) k"), AX.X,
                                ALU.max).then_inc(mx_ready.sem, 1)

            def normalise(g, i):
                dve.wait_ge(pv_done.sem, pv_done.at(g, i + 1))
                ps = B_M[:, 0:4 * PVW].rearrange("p (m c) -> p m c", c=PVW)
                V.reciprocal(r_sum[:, i], ps[:, :, 64:66]).then_inc(rsum_ready.sem, 1)
                dve.wait_ge(rsum_ready.sem, rsum_ready.at(g, i + 1))
                for ab in range(2):
                    rows = slice(C * ab, C * ab + C)
                    V.tensor_tensor(
                        o_n[rows, 2 * i:2 * i + 2, :].rearrange("p n (h j d) -> p (n h) j d", h=2, j=2),
                        ps[rows, :, 32 * ab:32 * ab + 32].rearrange("p m (j d) -> p m j d", j=2),
                        r_sum[rows, i].unsqueeze(3).broadcast_to([C, 4, 2, DH]), ALU.mult).then_inc(on_ready.sem, 1)

            def add_input(g, p):
                dve.wait_ge(proj_done.sem, proj_done.at(g, 1))
                first = (g % (2 * STRIPS)) // STRIPS * C
                planes = xt[:, bass.ds(first, C), bass.ds((g % STRIPS) * ROWS, ROWS)]
                V.tensor_tensor(x2[:, p].rearrange("p (k a) c -> p k a c", a=2),
                                B_M[:, :].rearrange("p (k a c) -> p k a c", a=2, c=C),
                                planes.rearrange("p c (a k) -> p k a c", a=2), ALU.add).then_inc(x2_ready.sem, 1)

            def token_mean(g, p):
                dve.wait_ge(x2_ready.sem, x2_ready.at(g, 1))
                V.tensor_reduce(ln[:, 0, :], x2[:, p], AX.X, ALU.add).then_inc(lsum.sem, 1)
                dve.wait_ge(lsum.sem, lsum.at(g, 1))
                V.tensor_scalar(ln[:, 1, :], ln[:, 0, :], 1.0 / C, None, ALU.mult).then_inc(lsum.sem, 1)

            def token_variance(g):
                dve.wait_ge(xc2_ready.sem, xc2_ready.at(g, 1))
                V.tensor_reduce(ln[:, 2, :], xc2[:, :, :], AX.X, ALU.add).then_inc(lvar.sem, 1)
                dve.wait_ge(lvar.sem, lvar.at(g, 1))
                V.tensor_scalar(ln[:, 2, :], ln[:, 2, :], 1.0 / C, LN_T_EPS, ALU.mult, ALU.add).then_inc(lvar.sem, 1)

            def over_experts(v):
                return v.unsqueeze(2).broadcast_to([P, ROWS, EXPERTS])

            def routing(g, first_step, last_step):
                lg, hot, first, rest, second = (rt[:, n] for n in range(5))
                gates = lg.rearrange("p (k a) e -> p k (a e)", a=2)
                top, next_top, gap, e, share, rank = (rs[:, n, :] for n in range(6))
                for step in range(first_step, last_step + 1):
                    if step == 0:
                        dve.wait_ge(logits_done.sem, logits_done.at(g, 1))
                        V.tensor_tensor(lg, B_P[:, 0:ROWS * EXPERTS].rearrange("p (r e) -> p r e", e=EXPERTS),
                                        b_rout[:, :, :], ALU.add).then_inc(route.sem, 1)
                        continue
                    dve.wait_ge(route.sem, route.at(g, step))
                    if step == 1:
                        V.tensor_reduce(top, lg, AX.X, ALU.max).then_inc(route.sem, 1)
                    elif step == 2:
                        V.tensor_tensor(hot, lg, over_experts(top), ALU.is_equal).then_inc(route.sem, 1)
                    elif step == 3:
                        V.tensor_tensor(hot, hot, e_rank[:, :, :], ALU.mult).then_inc(route.sem, 1)
                    elif step == 4:
                        V.tensor_reduce(rank, hot, AX.X, ALU.max).then_inc(route.sem, 1)
                    elif step == 5:
                        V.tensor_tensor(first, hot, over_experts(rank), ALU.is_equal).then_inc(route.sem, 1)
                    elif step == 6:
                        V.scalar_tensor_tensor(out=rest, in0=first, scalar=-3.0e38, in1=lg, op0=ALU.mult,
                                               op1=ALU.add).then_inc(route.sem, 1)
                    elif step == 7:
                        V.tensor_reduce(next_top, rest, AX.X, ALU.max).then_inc(route.sem, 1)
                    elif step == 8:
                        V.tensor_tensor(gap, next_top, top, ALU.subtract).then_inc(route.sem, 1)
                    elif step == 9:
                        V.tensor_tensor(hot, rest, over_experts(next_top), ALU.is_equal).then_inc(route.sem, 1)
                    elif step == 10:
                        V.tensor_tensor(hot, hot, e_rank[:, :, :], ALU.mult).then_inc(route.sem, 1)
                    elif step == 11:
                        V.tensor_reduce(rank, hot, AX.X, ALU.max).then_inc(route.sem, 1)
                    elif step == 12:
                        V.tensor_tensor(second, hot, over_experts(rank), ALU.is_equal).then_inc(route.sem, 1)
                    elif step == 13:
                        dve.wait_ge(e_ready.sem, e_ready.at(g, 1))
                        V.tensor_tensor(second, second, over_experts(e), ALU.mult).then_inc(route.sem, 1)
                    elif step == 14:
                        V.tensor_scalar(share, e, 1.0, None, ALU.add).then_inc(route.sem, 1)
                    elif step == 15:
                        V.reciprocal(share, share).then_inc(route.sem, 1)
                    elif step == 16:
                        V.tensor_tensor(lg, first, second, ALU.add).then_inc(route.sem, 1)
                    elif step == 17:
                        V.tensor_tensor(lg, lg, over_experts(share), ALU.mult).then_inc(route.sem, 1)
                    elif step == 18:
                        V.tensor_copy(g3[:, :, 0, :], gates).then_inc(route.sem, 1)
                    elif step == 19:
                        V.tensor_tensor(gates, gates, g3[:, :, 0, :], ALU.subtract).then_inc(route.sem, 1)
                    elif step == 20:
                        V.tensor_copy(g3[:, :, 1, :], gates).then_inc(route.sem, 1)
                    elif step == 21:
                        V.tensor_tensor(g3[:, :, 2, :], gates, g3[:, :, 1, :], ALU.subtract).then_inc(route.sem, 1)

            def gate(g, p, u):
                dve.wait_ge(gate_done.sem, gate_done.at(g, u + 1))
                dve.wait_ge(y_done.sem, y_done.at(g, max(u - TG + 1, 0)))
                V.tensor_tensor(t_g[:, u % TG, :], t_t[:, p, u % 2, :], B_G[:, :], ALU.mult).then_inc(tg_dve.sem, 1)

            def slot(j, p, group, on):
                projecting, attending, routing_on, mixing = (stage in on for stage in STAGES)
                if routing_on:
                    token_mean(j - 1, 1 - p)
                if attending:
                    bias_and_max(j, 0)
                    bias_and_max(j, 1)
                    bias_and_max(j, 2)
                if mixing:
                    gate(j - 2, p, 0)
                if routing_on:
                    token_variance(j - 1)
                if mixing:
                    gate(j - 2, p, 1)
                if attending:
                    bias_and_max(j, 3)
                if mixing:
                    gate(j - 2, p, 2)
                if attending:
                    normalise(j, 0)
                if projecting:
                    spread_values(j + 1, 1 - p, 0)
                if group and group[0] == "take":
                    take(group[1], group[2], p)
                if attending:
                    normalise(j, 1)
                if mixing:
                    gate(j - 2, p, 4)
                if routing_on:
                    routing(j - 1, 0, 2)
                if mixing:
                    gate(j - 2, p, 5)
                if routing_on:
                    routing(j - 1, 3, 4)
                if attending:
                    normalise(j, 2)
                if routing_on:
                    routing(j - 1, 5, 6)
                if mixing:
                    gate(j - 2, p, 6)
                if routing_on:
                    routing(j - 1, 7, 9)
                if attending:
                    normalise(j, 3)
                if routing_on:
                    routing(j - 1, 10, 21)
                if attending:
                    add_input(j, p)
                if projecting:
                    spread_values(j + 1, 1 - p, 1)

            pipeline(dve, slot, take, sum_up, lambda batch: None)

        @block.gpsimd
        def _(pool):
            G = nc.gpsimd
            G.memset(mhalf[:, :], -0.5).then_inc(set_pool.sem, 1)
            pool.wait_ge(set_pool.sem, 1)
            for p in range(2):
                G.memset(q_bd[:, p], 0.0).then_inc(set_pool.sem, 1)
                pool.wait_ge(set_pool.sem, 2 + p)
            pool.wait_ge(set_pool.sem, SET_POOL)

            def statistics(batch):
                par = batch % 2
                pool.wait_ge(rstd_ready.sem, rstd_ready.at(batch, RSTD_PARTS))
                G.tensor_tensor(m_rstd[:, bass.ds(par, 1), :].rearrange("p o h -> p (o h)"), st[:, 2, :],
                                rstd[:, bass.ds(par, 1), :].rearrange("p o h -> p (o h)"),
                                ALU.mult).then_inc(mr_ready.sem, 1)
                pool.wait_ge(mr_ready.sem, mr_ready.at(batch, 1))
                pool.sem_inc(passed, 1)

            def inverse_deviation(batch, part):
                cols = bass.ds(part * (H // RSTD_PARTS), H // RSTD_PARTS)
                pool.wait_ge(stat.sem, stat.at(batch, 6))
                pool.sem_inc(passed, 1)
                G.tensor_tensor(rstd[:, bass.ds(batch % 2, 1), cols].rearrange("p o h -> p (o h)"), st[:, 4, cols],
                                mhalf[:, 0:H // RSTD_PARTS], ALU.pow).then_inc(rstd_ready.sem, 1)

            def normalise_input(g):
                par = (g % (2 * STRIPS)) // STRIPS
                pool.wait_ge(qkv_done.sem, qkv_done.at(g))
                pool.sem_inc(passed, 1)
                G.tensor_tensor(xn[:, :, :], xt[:, bass.ds((g % (2 * STRIPS)) * 4, 4), :],
                                rstd[:, bass.ds(par, 1), :].broadcast_to([P, 4, H]), ALU.mult).then_inc(xn_ready.sem, 1)
                pool.wait_ge(xn_ready.sem, xn_ready.at(g, 1))
                G.tensor_tensor(xn[:, :, :], xn[:, :, :], m_rstd[:, bass.ds(par, 1), :].broadcast_to([P, 4, H]),
                                ALU.subtract).then_inc(xn_ready.sem, 1)

            def shift(g, i):
                pool.wait_ge(mx_ready.sem, mx_ready.at(g, i + 1))
                sc = prob[:, i].rearrange("p n h k -> p (n h) k")
                G.tensor_tensor(sc, sc, mx[:, i, :].unsqueeze(2).broadcast_to([P, 2 * HEADS, NTOK]),
                                ALU.subtract).then_inc(s_shifted.sem, 1)

            def over_c(v):
                return v.unsqueeze(2).broadcast_to([P, ROWS, C])

            def centre_tokens(g, p):
                pool.wait_ge(lsum.sem, lsum.at(g, 2))
                G.tensor_tensor(xc[:, :, :], x2[:, p], over_c(ln[:, 1, :]), ALU.subtract).then_inc(xc_ready.sem, 1)

            def scale_tokens(g):
                pool.wait_ge(lvar.sem, lvar.at(g, 2))
                G.tensor_tensor(ln[:, 3, :], ln[:, 2, :], mhalf[:, 0:ROWS], ALU.pow).then_inc(lrstd.sem, 1)
                pool.wait_ge(lrstd.sem, lrstd.at(g, 1))
                G.tensor_tensor(t_n[:, :, :], xc[:, :, :], over_c(ln[:, 3, :]), ALU.mult).then_inc(t_ready.sem, 1)

            def gate(g, p, u):
                n = ON_POOL.index(u)
                pool.wait_ge(g_copied.sem, g_copied.at(g, n + 1))
                pool.wait_ge(y_done.sem, y_done.at(g, max(u - TG + 1, 0)))
                G.tensor_tensor(t_g[:, u % TG, :], t_t[:, p, u % 2, :], g_copy[:, n % 2, :],
                                ALU.mult).then_inc(tg_pool.sem, 1)

            def slot(j, p, group, on):
                projecting, attending, routing_on, mixing = (stage in on for stage in STAGES)
                if routing_on:
                    centre_tokens(j - 1, 1 - p)
                if attending:
                    shift(j, 0)
                    shift(j, 1)
                    shift(j, 2)
                if routing_on:
                    scale_tokens(j - 1)
                if projecting and not (isinstance(j, int) and j == LAST - 1):
                    normalise_input(j + 2)
                if attending:
                    shift(j, 3)
                if mixing:
                    gate(j - 2, p, 3)
                if group and group[0] == "power":
                    inverse_deviation(group[1], group[2])
                if mixing:
                    gate(j - 2, p, 7)

            def first_statistics(batch):
                statistics(batch)
                if isinstance(batch, int):
                    normalise_input(0)

            pipeline(pool, slot, lambda batch, t, r: None, lambda batch: None, first_statistics)


SET_DVE = 10 + 2 + 3 * PARTS - 1
PART_ROWS = (0, 32, 64)
SET_POOL = 3
LAST = BATCH * STRIPS - 1
ROUTE_GAP = 9


def rel_index():
    m = np.arange(NTOK)
    r, c = m // 4 % 8, 2 * (m % 4) + m // 32
    return (m[:, None] // WS - r[None, :] + WS - 1) * (2 * WS - 1) + m[:, None] % WS - c[None, :] + WS - 1


_SHAPE = (BATCH, C, H, W)


def kernel(x, L0_conv_Wq, L0_conv_bq, L0_conv_Wkv, L0_conv_bkv, L0_conv_rel_bias, L0_conv_Wproj, L0_conv_bproj,
           L0_ffn_router_w, L0_ffn_router_b, L0_ffn_expert_w, L0_ffn_expert_b):
    import concourse.bacc as _bacc
    from concourse.bass_utils import run_bass_kernel_spmd as _run

    f = np.float32
    a = {k: np.asarray(v) for k, v in dict(
        x=x, wq=L0_conv_Wq, bq=L0_conv_bq, wkv=L0_conv_Wkv, bkv=L0_conv_bkv, rel=L0_conv_rel_bias, wp=L0_conv_Wproj,
        bp=L0_conv_bproj, rw=L0_ffn_router_w, rb=L0_ffn_router_b, ew=L0_ffn_expert_w, eb=L0_ffn_expert_b).items()}
    wqkv = np.concatenate([a["wq"][:, None], a["wkv"].reshape(C, 2, C)], 1)
    qkvb = np.concatenate([a["bq"][:, None], a["bkv"].reshape(2, C).T], 1)
    zero = np.zeros_like(wqkv)
    no_proj = np.zeros_like(a["wp"])
    bproj = np.zeros((C + 1, ROWS, C), f)
    bproj[list(PART_ROWS)] = a["bp"]
    no_router = np.zeros_like(a["rw"])
    wexp = a["ew"].reshape(MIXES // 2, 2, C, C).transpose(1, 2, 0, 3).reshape(P, MIXES // 2, C)
    bexp = np.zeros((PARTS, 2, EXPERTS, 2, C), f)
    sel = np.zeros((PARTS, 2, EXPERTS, MIXES, 2, C), f)
    for g in range(2):
        bexp[:, g, :, g, :] = a["eb"]
        for e in range(EXPERTS):
            sel[:, g, e, e // 2 * 2 + g, e % 2, :] = 1.0
    kmask = np.zeros((2, HEADS, DH, HEADS), f)
    kbias = np.zeros((2, HEADS, DH, HEADS), f)
    for h in range(HEADS):
        kmask[:, h, :, h] = 1.0
        kbias[:, h, :, h] = a["bkv"][:C].reshape(HEADS, DH)[h]
    relb = a["rel"][rel_index()].transpose(0, 2, 1).reshape(NTOK, HEADS * NTOK)
    arrays = {
        "x": a["x"],
        "wqkv": np.stack([np.concatenate([wqkv, zero]), np.concatenate([zero, wqkv])], 1),
        "qkvb": np.concatenate([qkvb, qkvb]),
        "kmask": kmask.reshape(P, HEADS),
        "kbias": kbias.reshape(P, HEADS),
        "wproj": np.stack([np.concatenate([a["wp"], no_proj]), np.concatenate([no_proj, a["wp"]])], 1),
        "wrout": np.concatenate([np.concatenate([a["rw"], no_router], 1), np.concatenate([no_router, a["rw"]], 1)]),
        "brout": np.broadcast_to(a["rb"], (P, ROWS, EXPERTS)),
        "wexp": wexp,
        "bexp": bexp.reshape(GROWS, P),
        "relb": np.concatenate([relb, relb]),
        "ident": np.eye(P, dtype=f),
        "sel": sel.reshape(GROWS, MIXES, P),
        "rank": np.broadcast_to(np.arange(EXPERTS, 0, -1, dtype=f), (P, ROWS, EXPERTS)),
        "bproj": bproj.reshape(C + 1, BANK),
    }
    arrays = {k: np.ascontiguousarray(v) for k, v in arrays.items()}
    nc = _bacc.Bacc("TRN2", target_bir_lowering=False, num_devices=1)
    args = [nc.dram_tensor(f"in_{k}", v.shape, F32, kind="ExternalInput").ap() for k, v in arrays.items()]
    out = nc.dram_tensor("out_y", _SHAPE, F32, kind="ExternalOutput").ap()
    build(nc, *args, out)
    r = _run(nc, [{f"in_{k}": v for k, v in arrays.items()}], core_ids=[0])
    return r.results[0]["out_y"]
```
